# Optimizing a Trainium2 kernel written in Bass

```python
import numpy as np
import jax
import jax.numpy as jnp

def _softmax(x, axis=-1):
    return jax.nn.softmax(x, axis=axis)

def _gelu(x):
    return jax.nn.gelu(x, approximate=True)

def _silu(x):
    return jax.nn.silu(x)

def _sigmoid(x):
    return jax.nn.sigmoid(x)

def _layernorm(x, axis=-1, eps=1e-05):
    m = jnp.mean(x, axis=axis, keepdims=True)
    v = jnp.var(x, axis=axis, keepdims=True)
    return (x - m) / jnp.sqrt(v + eps)

def _scatter_add(tgt, idx, src, axis=0):
    return tgt.at[idx].add(src)

def _segment_sum(src, seg, n):
    return jax.ops.segment_sum(src, seg, n)
kernel_name = 'mk_adaln_ffn_d2_seqx_r8_fba824'

def setup_inputs(seed: int=0):
    np.random.seed(seed)
    _w = jnp.asarray

    def _rec_inputs():
        import jax
        import jax.numpy as jnp
        _rk = jax.random.key(seed)
        x = -0.000125 + 0.9999 * jax.random.normal(jax.random.fold_in(_rk, 1), (4, 256, 256), jnp.float32)
        _lenS = 256 - jax.random.randint(jax.random.fold_in(_rk, 7), (4,), 0, max(1, 256 // 4) + 1, jnp.int32)
        _lenS2 = 256 - jax.random.randint(jax.random.fold_in(_rk, 8), (4,), 0, max(1, 256 // 4) + 1, jnp.int32)
        fside_BxSxS_0 = -1.52775e-05 + 0.999936 * jax.random.normal(jax.random.fold_in(_rk, 11), (4, 256, 256), jnp.float32)
        cond_512 = -5.03954e-05 + 1.00559 * jax.random.normal(jax.random.fold_in(_rk, 12), (4, 64), jnp.float32)
        return (x, fside_BxSxS_0, cond_512)
    x, fside_BxSxS_0, cond_512 = _rec_inputs()

    def _L0_cond_setup():
        import jax, jax.numpy as jnp
        from jax import lax
        import numpy as np
        B, T, C, TD = (8, 256, 256, 64)

        def _bi_wkv(r, k, v, w, u, time_emb):
            tf = jax.nn.sigmoid(jnp.sum(time_emb, axis=-1))[:, None, None]
            decay = jnp.exp(-jnp.exp(w.astype(jnp.float32)))[None, :] * (0.5 + 0.5 * tf[:, :, 0])
            kf = k.astype(jnp.float32)
            vf = v.astype(jnp.float32)
            ek = jnp.exp(jnp.minimum(kf, 30.0))
            ekv = ek * vf

            def step(carry, x):
                a, b = carry
                ekv_t, ek_t = x
                a = a * decay + ekv_t
                b = b * decay + ek_t
                return ((a, b), (a, b))
            ekv_t = jnp.swapaxes(ekv, 0, 1)
            ek_t = jnp.swapaxes(ek, 0, 1)
            init = (jnp.zeros_like(decay), jnp.zeros_like(decay))
            _, (nf, df) = lax.scan(step, init, (ekv_t, ek_t))
            _, (nb, db) = lax.scan(step, init, (ekv_t, ek_t), reverse=True)
            nf = jnp.swapaxes(nf, 0, 1)
            df = jnp.swapaxes(df, 0, 1)
            nb = jnp.swapaxes(nb, 0, 1)
            db = jnp.swapaxes(db, 0, 1)
            euk = jnp.exp(jnp.minimum(u.astype(jnp.float32)[None, None, :] + kf, 30.0))
            num = nf + nb - ekv + euk * vf
            den = df + db - ek + euk
            base = jax.nn.sigmoid(r.astype(jnp.float32)) * (num / jnp.maximum(den, 1e-08))
            out = base * (0.8 + 0.2 * tf)
            return out.astype(r.dtype)
        key = jax.random.key(seed)
        ks = jax.random.split(key, 6)
        return {'r': jax.random.normal(ks[0], (B, T, C), dtype=jnp.float32), 'k': jax.random.normal(ks[1], (B, T, C), dtype=jnp.float32), 'v': jax.random.normal(ks[2], (B, T, C), dtype=jnp.float32), 'w': jax.random.normal(ks[3], (C,), dtype=jnp.float32), 'u': jax.random.normal(ks[4], (C,), dtype=jnp.float32), 'time_emb': jax.random.normal(ks[5], (B, TD), dtype=jnp.float32)}
    _L0_cond_all = _L0_cond_setup()
    _L0_cond_in = {k: v for k, v in _L0_cond_all.items() if k in ('w', 'u')}
    del _L0_cond_all

    def _L0_ffn_setup():
        import jax, jax.numpy as jnp
        import numpy as np
        B, S, D, R, E = (4, 256, 256, 64, 8)
        SCALING = 64.0 / 16.0
        key = jax.random.key(seed)
        k1, k2, k3, k4 = jax.random.split(key, 4)
        x = jax.random.normal(k1, (B, S, D), dtype=jnp.float32)
        A = jax.random.normal(k2, (E, R, D), dtype=jnp.float32) * 0.02
        Bw = jax.random.normal(k3, (E, D, R), dtype=jnp.float32) * 0.02
        Wg = jax.random.normal(k4, (E, D), dtype=jnp.float32) * 0.02
        return {'x': x, 'A': A, 'Bw': Bw, 'Wg': Wg}
    _L0_ffn_all = _L0_ffn_setup()
    _L0_ffn_in = {k: v for k, v in _L0_ffn_all.items() if k in ('A', 'Bw', 'Wg')}
    del _L0_ffn_all

    def _L1_cond_setup():
        import jax, jax.numpy as jnp
        from jax import lax
        import numpy as np
        B, T, C, TD = (8, 256, 256, 64)

        def _bi_wkv(r, k, v, w, u, time_emb):
            tf = jax.nn.sigmoid(jnp.sum(time_emb, axis=-1))[:, None, None]
            decay = jnp.exp(-jnp.exp(w.astype(jnp.float32)))[None, :] * (0.5 + 0.5 * tf[:, :, 0])
            kf = k.astype(jnp.float32)
            vf = v.astype(jnp.float32)
            ek = jnp.exp(jnp.minimum(kf, 30.0))
            ekv = ek * vf

            def step(carry, x):
                a, b = carry
                ekv_t, ek_t = x
                a = a * decay + ekv_t
                b = b * decay + ek_t
                return ((a, b), (a, b))
            ekv_t = jnp.swapaxes(ekv, 0, 1)
            ek_t = jnp.swapaxes(ek, 0, 1)
            init = (jnp.zeros_like(decay), jnp.zeros_like(decay))
            _, (nf, df) = lax.scan(step, init, (ekv_t, ek_t))
            _, (nb, db) = lax.scan(step, init, (ekv_t, ek_t), reverse=True)
            nf = jnp.swapaxes(nf, 0, 1)
            df = jnp.swapaxes(df, 0, 1)
            nb = jnp.swapaxes(nb, 0, 1)
            db = jnp.swapaxes(db, 0, 1)
            euk = jnp.exp(jnp.minimum(u.astype(jnp.float32)[None, None, :] + kf, 30.0))
            num = nf + nb - ekv + euk * vf
            den = df + db - ek + euk
            base = jax.nn.sigmoid(r.astype(jnp.float32)) * (num / jnp.maximum(den, 1e-08))
            out = base * (0.8 + 0.2 * tf)
            return out.astype(r.dtype)
        key = jax.random.key(seed)
        ks = jax.random.split(key, 6)
        return {'r': jax.random.normal(ks[0], (B, T, C), dtype=jnp.float32), 'k': jax.random.normal(ks[1], (B, T, C), dtype=jnp.float32), 'v': jax.random.normal(ks[2], (B, T, C), dtype=jnp.float32), 'w': jax.random.normal(ks[3], (C,), dtype=jnp.float32), 'u': jax.random.normal(ks[4], (C,), dtype=jnp.float32), 'time_emb': jax.random.normal(ks[5], (B, TD), dtype=jnp.float32)}
    _L1_cond_all = _L1_cond_setup()
    _L1_cond_in = {k: v for k, v in _L1_cond_all.items() if k in ('w', 'u')}
    del _L1_cond_all

    def _L1_ffn_setup():
        import jax, jax.numpy as jnp
        import numpy as np
        D_MODEL = 256
        D_FF = 1024

        def absmean_quant(w):
            scale = jnp.mean(jnp.abs(w))
            mask = (jnp.abs(w) >= scale * 0.7).astype(w.dtype)
            return jnp.sign(w) * mask
        key = jax.random.key(seed)
        k_x, k_w1, k_w2 = jax.random.split(key, 3)
        x = jax.random.normal(k_x, (4, 512, D_MODEL), dtype=jnp.float32)
        w1 = jax.random.normal(k_w1, (D_FF, D_MODEL), dtype=jnp.float32)
        b1 = jnp.zeros((D_FF,), dtype=jnp.float32)
        w2 = jax.random.normal(k_w2, (D_MODEL, D_FF), dtype=jnp.float32)
        b2 = jnp.zeros((D_MODEL,), dtype=jnp.float32)
        return {'x': x, 'w1': w1, 'b1': b1, 'w2': w2, 'b2': b2}
    _L1_ffn_all = _L1_ffn_setup()
    _L1_ffn_in = {k: v for k, v in _L1_ffn_all.items() if k in ('w1', 'b1', 'w2', 'b2')}
    del _L1_ffn_all
    return {'x': x, 'fside_BxSxS_0': fside_BxSxS_0, 'cond_512': cond_512, 'L0_cond_w': _L0_cond_in['w'], 'L0_cond_u': _L0_cond_in['u'], 'L0_ffn_A': _L0_ffn_in['A'], 'L0_ffn_Bw': _L0_ffn_in['Bw'], 'L0_ffn_Wg': _L0_ffn_in['Wg'], 'L1_cond_w': _L1_cond_in['w'], 'L1_cond_u': _L1_cond_in['u'], 'L1_ffn_w1': _L1_ffn_in['w1'], 'L1_ffn_b1': _L1_ffn_in['b1'], 'L1_ffn_w2': _L1_ffn_in['w2'], 'L1_ffn_b2': _L1_ffn_in['b2']}

def reference(x, fside_BxSxS_0, cond_512, L0_cond_w, L0_cond_u, L0_ffn_A, L0_ffn_Bw, L0_ffn_Wg, L1_cond_w, L1_cond_u, L1_ffn_w1, L1_ffn_b1, L1_ffn_w2, L1_ffn_b2):
    import jax
    import jax.numpy as jnp

    def _L0_cond_ref(r, k, v, w, u, time_emb):
        import jax, jax.numpy as jnp
        from jax import lax
        import numpy as np
        B, T, C, TD = (8, 256, 256, 64)

        def _bi_wkv(r, k, v, w, u, time_emb):
            tf = jax.nn.sigmoid(jnp.sum(time_emb, axis=-1))[:, None, None]
            decay = jnp.exp(-jnp.exp(w.astype(jnp.float32)))[None, :] * (0.5 + 0.5 * tf[:, :, 0])
            kf = k.astype(jnp.float32)
            vf = v.astype(jnp.float32)
            ek = jnp.exp(jnp.minimum(kf, 30.0))
            ekv = ek * vf

            def step(carry, x):
                a, b = carry
                ekv_t, ek_t = x
                a = a * decay + ekv_t
                b = b * decay + ek_t
                return ((a, b), (a, b))
            ekv_t = jnp.swapaxes(ekv, 0, 1)
            ek_t = jnp.swapaxes(ek, 0, 1)
            init = (jnp.zeros_like(decay), jnp.zeros_like(decay))
            _, (nf, df) = lax.scan(step, init, (ekv_t, ek_t))
            _, (nb, db) = lax.scan(step, init, (ekv_t, ek_t), reverse=True)
            nf = jnp.swapaxes(nf, 0, 1)
            df = jnp.swapaxes(df, 0, 1)
            nb = jnp.swapaxes(nb, 0, 1)
            db = jnp.swapaxes(db, 0, 1)
            euk = jnp.exp(jnp.minimum(u.astype(jnp.float32)[None, None, :] + kf, 30.0))
            num = nf + nb - ekv + euk * vf
            den = df + db - ek + euk
            base = jax.nn.sigmoid(r.astype(jnp.float32)) * (num / jnp.maximum(den, 1e-08))
            out = base * (0.8 + 0.2 * tf)
            return out.astype(r.dtype)
        return _bi_wkv(r, k, v, w, u, time_emb)

    def _L0_ffn_ref(x, A, Bw, Wg):
        import jax, jax.numpy as jnp
        import numpy as np
        B, S, D, R, E = (4, 256, 256, 64, 8)
        SCALING = 64.0 / 16.0
        bsz, seq_len, dim = x.shape
        xf = x.reshape(-1, dim)
        logits = jnp.einsum('nd,ed->ne', xf, Wg)
        prob = jax.nn.softmax(logits, axis=-1)
        gate = jnp.argmax(prob, axis=-1)
        prob_sel = jnp.take_along_axis(prob, gate[:, None], axis=1)
        mask = jax.nn.one_hot(gate, E, dtype=xf.dtype)
        h = jnp.einsum('nd,erd->ner', xf, A)
        h = h * mask[:, :, None]
        y = jnp.einsum('ner,eor->no', h, Bw)
        y = y * SCALING * prob_sel
        return y.reshape(bsz, seq_len, -1)

    def _L1_cond_ref(r, k, v, w, u, time_emb):
        import jax, jax.numpy as jnp
        from jax import lax
        import numpy as np
        B, T, C, TD = (8, 256, 256, 64)

        def _bi_wkv(r, k, v, w, u, time_emb):
            tf = jax.nn.sigmoid(jnp.sum(time_emb, axis=-1))[:, None, None]
            decay = jnp.exp(-jnp.exp(w.astype(jnp.float32)))[None, :] * (0.5 + 0.5 * tf[:, :, 0])
            kf = k.astype(jnp.float32)
            vf = v.astype(jnp.float32)
            ek = jnp.exp(jnp.minimum(kf, 30.0))
            ekv = ek * vf

            def step(carry, x):
                a, b = carry
                ekv_t, ek_t = x
                a = a * decay + ekv_t
                b = b * decay + ek_t
                return ((a, b), (a, b))
            ekv_t = jnp.swapaxes(ekv, 0, 1)
            ek_t = jnp.swapaxes(ek, 0, 1)
            init = (jnp.zeros_like(decay), jnp.zeros_like(decay))
            _, (nf, df) = lax.scan(step, init, (ekv_t, ek_t))
            _, (nb, db) = lax.scan(step, init, (ekv_t, ek_t), reverse=True)
            nf = jnp.swapaxes(nf, 0, 1)
            df = jnp.swapaxes(df, 0, 1)
            nb = jnp.swapaxes(nb, 0, 1)
            db = jnp.swapaxes(db, 0, 1)
            euk = jnp.exp(jnp.minimum(u.astype(jnp.float32)[None, None, :] + kf, 30.0))
            num = nf + nb - ekv + euk * vf
            den = df + db - ek + euk
            base = jax.nn.sigmoid(r.astype(jnp.float32)) * (num / jnp.maximum(den, 1e-08))
            out = base * (0.8 + 0.2 * tf)
            return out.astype(r.dtype)
        return _bi_wkv(r, k, v, w, u, time_emb)

    def _L1_ffn_ref(x, w1, b1, w2, b2):
        import jax, jax.numpy as jnp
        import numpy as np
        D_MODEL = 256
        D_FF = 1024

        def absmean_quant(w):
            scale = jnp.mean(jnp.abs(w))
            mask = (jnp.abs(w) >= scale * 0.7).astype(w.dtype)
            return jnp.sign(w) * mask
        w1_q = absmean_quant(w1)
        w2_q = absmean_quant(w2)
        h = jnp.einsum('bsd,fd->bsf', x, w1_q) + b1
        h = jax.nn.gelu(h, approximate=False)
        out = jnp.einsum('bsf,df->bsd', h, w2_q) + b2
        return out
    x = x + _L0_ffn_ref(_L0_cond_ref(x, fside_BxSxS_0, fside_BxSxS_0, L0_cond_w, L0_cond_u, cond_512), L0_ffn_A, L0_ffn_Bw, L0_ffn_Wg)
    x = x + _L1_ffn_ref(_L1_cond_ref(x, fside_BxSxS_0, fside_BxSxS_0, L1_cond_w, L1_cond_u, cond_512), L1_ffn_w1, L1_ffn_b1, L1_ffn_w2, L1_ffn_b2)
    return x

_drawn_inputs = setup_inputs


def setup_inputs(seed=0):
    import zlib

    import numpy as np

    out = dict(_drawn_inputs(seed))
    spreads = {'L1_ffn_b1': (0.0, 0.475), 'L1_ffn_b2': (0.0, 0.8)}
    factors = {'L0_cond_w': 8.0, 'L0_cond_u': 8.0, 'L0_ffn_A': 8.0, 'L0_ffn_Bw': 8.0, 'L0_ffn_Wg': 8.0}
    for name, (base, spread) in spreads.items():
        noise = np.random.default_rng([zlib.crc32(name.encode()), seed]).standard_normal(out[name].shape)
        drawn = base * np.exp(spread * noise) if base else spread * noise
        out[name] = jnp.asarray(drawn.astype(out[name].dtype))
    for name, factor in factors.items():
        out[name] = (out[name] * factor).astype(out[name].dtype)
    return out
```

```python
from contextlib import ExitStack

import concourse.bass as bass
from concourse import mybir

ALU = mybir.AluOpType
ACT = mybir.ActivationFunctionType
F32 = mybir.dt.float32
F32R = mybir.dt.float32r
BF16 = mybir.dt.bfloat16
U32 = mybir.dt.uint32
AX_X = mybir.AxisListType.X

P = 128
EXP30 = 1.0686474581524463e13


def adaln_ffn_kernel(nc, x, fside, cond, w_l0, u_l0, A, Bw, Wg, w_l1, u_l1, w1, b1, w2, b2, out):
    NB, T, C = x.shape
    NE, R, _ = A.shape
    DFF = w1.shape[0]
    TD = cond.shape[1]
    NC = C // P
    NT = T // P
    NI = NB * NT
    ER = NE * R
    NM = ER // P
    NF = DFF // P
    NJ = NF // 2
    NV = 4 * NC + NF
    LAYERS = 2
    EXTRA_SCALE = 4.0
    assert NC == 2 and NT == 2 and ER == 512 and NF == 8 and NB == 4

    with ExitStack() as ctx:
        def sb(name, shape, dt=F32, where=ctx):
            return where.enter_context(nc.sbuf_tensor(name, shape, dt))

        def sem(name):
            return ctx.enter_context(nc.semaphore(name))

        bank = [ctx.enter_context(nc.psum_tensor(f"bank{k}", [P, 512], F32)) for k in range(8)]

        ident = sb("ident", [P, P])
        identb = sb("identb", [P, P], BF16)
        ones = sb("ones", [P, P])
        iota8 = sb("iota8", [P, NE])
        vec_rows = sb("vec_rows", [NV, P])
        vecs = sb("vecs", [P, NV])
        cond_all = sb("cond_all", [P, NB, TD])
        tf = sb("tf", [P, 3, NB])
        out_scale = sb("out_scale", [P, 2, NB])
        edecay = sb("edecay", [P, LAYERS, NC])
        decay = sb("decay", [P, LAYERS, NC, NB])
        one_less_d2 = sb("one_less_d2", [P, LAYERS, NC, NB])
        b2_all = sb("b2_all", [P, C])
        x_nat = sb("x_nat", [P, NI, C])
        x1b = sb("x1b", [P, NI, C])
        FT = sb("FT", [P, NB, NC, T])
        kv = sb("kv", [P, NB, NC, 2, T])
        euk = sb("euk", [P, NB, NC, T])
        scan1 = sb("scan1", [P, NB, NC, 2, T])
        nd = [sb(f"nd{l}", [P, NB, NC, 2, T]) for l in range(LAYERS)]
        sig = sb("sig", [P, NB, NC, T])
        xin_hi = sb("xin_hi", [P, 2, NC, T], F32R)
        xin_lo = sb("xin_lo", [P, 2, NC, T], F32R)
        WgT = sb("WgT", [P, NC, NE])
        AT = sb("AT", [P, NC, ER])
        BT = sb("BT", [P, NM, C])
        w1T = sb("w1T", [P, NC, DFF], F32R)
        w2T = sb("w2T", [P, NF, C], F32R)
        q1 = sb("q1", [P, NF, C], BF16)
        q2 = sb("q2", [P, NC, DFF], BF16)
        wsum = sb("wsum", [P, 2])
        thr = sb("thr", [P, 2, 2])
        mx8 = sb("mx8", [P, NI, NE])
        idx8 = sb("idx8", [P, NI, NE], U32)
        negmax = sb("negmax", [P, NI])
        logits = sb("logits", [P, NI, NE])
        gexp = sb("gexp", [P, NI, NE])
        gsum = sb("gsum", [P, NI])
        grec = sb("grec", [P, NI])
        mask = sb("mask", [P, NI, NE])
        hm = sb("hm", [P, 2, ER])
        hmT = sb("hmT", [P, 2, NM, P])
        h32 = sb("h32", [P, NF, T])
        outb = sb("outb", [P, 2, C])
        early = ExitStack()
        F_nat = sb("F_nat", [P, NB, NT, C], F32, early)
        w1_nat = sb("w1_nat", [P, NF, C], F32, early)
        w2_nat = sb("w2_nat", [P, NC, DFF], F32, early)
        A_nat = sb("A_nat", [P, NM, C], F32, early)
        B_nat = sb("B_nat", [P, NC, NE, R], F32, early)
        Wg_nat = sb("Wg_nat", [NE, C], F32, early)
        neg_part = sb("neg_part", [P, 2 * DFF], BF16, early)
        early.close()
        h_hi = sb("h_hi", [P, 2, NF, T], F32R)
        h_lo = sb("h_lo", [P, 2, NF, T], F32R)

        def per(kind, n):
            return [sem(f"{kind}_{k}") for k in range(n)]

        def nth(l, b):
            return NB * l + b

        F_loaded, x_loaded = per("F_loaded", NB), per("x_loaded", NB)
        vec_loaded, cond_loaded, b2_loaded = sem("vec_loaded"), sem("cond_loaded"), sem("b2_loaded")
        Wg_loaded, A_loaded, B_loaded = sem("Wg_loaded"), sem("A_loaded"), sem("B_loaded")
        w_loaded = per("w_loaded", 2)
        consts_ready, identb_ready = sem("consts_ready"), sem("identb_ready")
        FT_psum, xT_psum = sem("FT_psum"), sem("xT_psum")
        vec_psum, vecs_ready = sem("vec_psum"), sem("vecs_ready")
        small_dve, small_act, decay_ready = sem("small_dve"), sem("small_act"), sem("decay_ready")
        ek_exp, ekv_ready, kv_ready = sem("ek_exp"), sem("ekv_ready"), sem("kv_ready")
        FT_ready, sig_ready = sem("FT_ready"), sem("sig_ready")
        euk_ready = sem("euk_ready")
        fwd_done, scaled, bwd_done = sem("fwd_done"), sem("scaled"), sem("bwd_done")
        den_ready, eukv_ready, num_ready = sem("den_ready"), sem("eukv_ready"), sem("num_ready")
        ln_done, rec_ready = sem("ln_done"), sem("rec_ready")
        dr_ready, q_ready, ratio_ready = sem("dr_ready"), sem("q_ready"), sem("ratio_ready")
        cond_ready = sem("cond_ready")
        Wg_psum, A_psum, B_psum = sem("Wg_psum"), sem("A_psum"), sem("B_psum")
        WgT_ready, AT_ready, BT_ready = sem("WgT_ready"), sem("AT_ready"), sem("BT_ready")
        wsum_ready, wtot_psum, thr_ready = sem("wsum_ready"), sem("wtot_psum"), sem("thr_ready")
        neg_ready, quant_ready = sem("neg_ready"), sem("quant_ready")
        qT_psum, wT_ready = sem("qT_psum"), sem("wT_ready")
        logits_ready = sem("logits_ready")
        logits_psum, h_psum = sem("logits_psum"), sem("h_psum")
        max_ready, negmax_ready, idx_ready = sem("max_ready"), sem("negmax_ready"), sem("idx_ready")
        mask_ready, gsum_ready, grec_ready = sem("mask_ready"), sem("gsum_ready"), sem("grec_ready")
        hm_ready, hmT_psum, hmT_ready = sem("hm_ready"), sem("hmT_psum"), sem("hmT_ready")
        y_psum, x1_ready, x1b_ready = sem("y_psum"), sem("x1_ready"), sem("x1b_ready")
        x1T_psum, tanh_ready, xin_ready = sem("x1T_psum"), sem("tanh_ready"), sem("xin_ready")
        xhi_ready, xlo_ready = sem("xhi_ready"), sem("xlo_ready")
        g_psum, h32_ready, hhi_ready, hlo_ready = sem("g_psum"), sem("h32_ready"), sem("hhi_ready"), sem("hlo_ready")
        o_psum, out_ready = sem("o_psum"), sem("out_ready")
        out_stored = per("out_stored", 2)

        F_bank = [0, 1, 7, 0]
        x_bank = [2, 3, 4, 5]
        A_bank, B_bank = [1, 2], [3, 4]
        WT_BANK = 7
        x1T_bank = [6, 7]
        HMT_BANK, H_BANK, Y_BANK, MISC_BANK = 0, 2, 4, 6
        TOTAL_AT = (2, 4)
        WT_AT = (4, 5, 7, 8)
        VEC_AT, WG_AT, WTOT_AT, LOGIT_AT = 0, 32, 64, 128

        def chunked(k):
            return bank[k][:, :].rearrange("p (c t) -> p c t", c=NC)

        def ratio_products(eng, l, b):
            num, den = nd[l][:, b, :, 0, :], nd[l][:, b, :, 1, :]
            rec, dr = scan1[:, b, :, 0, :], scan1[:, b, :, 1, :]
            eng.wait_ge(bwd_done, 2 * NC * nth(l, b) + 2 * NC)
            eng.wait_ge(eukv_ready, nth(l, b) + 1)
            eng.tensor_tensor(num, num, euk[:, b], ALU.add).then_inc(num_ready, 1)
            eng.wait_ge(den_ready, nth(l, b) + 1)
            eng.wait_ge(rec_ready, nth(l, b) + 1)
            eng.tensor_tensor(dr, den, rec, ALU.mult).then_inc(dr_ready, 1)
            eng.wait_ge(num_ready, nth(l, b) + 1)
            eng.tensor_tensor(num, num, rec, ALU.mult).then_inc(q_ready, 1)

        block = ctx.enter_context(nc.Block())

        @block.sync
        def _(sp):
            for k, v in enumerate((w_l0, u_l0, w_l1, u_l1)):
                sp.dma_start(vec_rows[NC * k:NC * (k + 1), :], v.rearrange("(c p) -> c p", p=P)).then_inc(vec_loaded, 16)
            F_tiles = fside.rearrange("b (n p) c -> b p n c", p=P)
            x_tiles = x.rearrange("b (n p) c -> b p n c", p=P)
            sp.dma_start(F_nat[:, 1], F_tiles[1]).then_inc(F_loaded[1], 16)
            for b in range(NB):
                sp.dma_start(x_nat[:, NT * b:NT * (b + 1)], x_tiles[b]).then_inc(x_loaded[b], 16)
            for b in range(2, NB):
                sp.dma_start(F_nat[:, b], F_tiles[b]).then_inc(F_loaded[b], 16)
            sp.dma_start(A_nat[:, :, :], A.rearrange("e r c -> (e r) c").rearrange("(m p) c -> p m c", p=P)).then_inc(A_loaded, 16)
            for c in range(NC):
                sp.dma_start(B_nat[:, c], Bw[:, c * P:(c + 1) * P, :].rearrange("e o r -> o e r")).then_inc(B_loaded, 16)
            sp.dma_start(w1_nat[:, :, :], w1.rearrange("(n p) c -> p n c", p=P)).then_inc(w_loaded[0], 16)
            sp.dma_start(w2_nat[:, :, :], w2.rearrange("(n p) f -> p n f", p=P)).then_inc(w_loaded[1], 16)
            sp.dma_start(b2_all[:, :], b2.rearrange("(a n) -> a n", a=1).broadcast_to([P, C])).then_inc(b2_loaded, 16)
            out_tiles = out.rearrange("b (n p) c -> (b n) p c", p=P)
            for i in range(NI):
                sp.wait_ge(out_ready, i + 1)
                sp.dma_start(out_tiles[i], outb[:, i % 2]).then_inc(out_stored[i % 2], 16)
            for k in range(2):
                sp.wait_ge(out_stored[k], 16 * NI // 2)

        @block.gpsimd
        def _(pool):
            pool.memset(ident[:, :], 0.0).then_inc(consts_ready, 1)
            pool.wait_ge(consts_ready, 1)
            pool.affine_select(out=ident[:, :], in_=ident[:, :], compare_op=ALU.not_equal, fill=1.0, base=0,
                               pattern=[[-1, P]], channel_multiplier=1).then_inc(consts_ready, 1)
            pool.memset(ones[:, :], 1.0).then_inc(consts_ready, 1)
            for e in range(NE):
                pool.memset(iota8[:, e:e + 1], float(e)).then_inc(consts_ready, 1)

            def negatives(k):
                pool.wait_ge(thr_ready, 2 * (k + 1))
                if k:
                    pool.wait_ge(quant_ready, k)
                flat = (w1_nat if k == 0 else w2_nat)[:, :, :].rearrange("p a b -> p (a b)")
                pool.tensor_scalar(neg_part[:, :], flat, thr[:, k, 1:2], None, ALU.is_le).then_inc(neg_ready, 1)

            def add_b2(i):
                pool.wait_ge(b2_loaded, 16)
                pool.wait_ge(x1_ready, i + 1)
                pool.tensor_tensor(x1b[:, i], x_nat[:, i], b2_all[:, :], ALU.add).then_inc(x1b_ready, 1)

            for b in range(1, NB):
                ratio_products(pool, 0, b)
            negatives(0)
            negatives(1)
            for b in range(0, NB):
                ratio_products(pool, 1, b)
                add_b2(2 * b)
                add_b2(2 * b + 1)

        @block.scalar
        def _(act):
            F_tiles = fside.rearrange("b (n p) c -> b p n c", p=P)
            act.dma_start(F_nat[:, 0], F_tiles[0]).then_inc(F_loaded[0], 16)
            act.dma_start(cond_all[:, :, :].rearrange("p b d -> p (b d)"),
                          cond.rearrange("b d -> (b d)").rearrange("(a n) -> a n", a=1).broadcast_to([P, NB * TD])).then_inc(cond_loaded, 16)
            act.dma_start(vec_rows[4 * NC:NV, :], b1.rearrange("(c p) -> c p", p=P)).then_inc(vec_loaded, 16)
            act.dma_start(Wg_nat[:, :], Wg).then_inc(Wg_loaded, 16)

            act.wait_ge(small_dve, 1)
            act.activation(tf[:, 1], tf[:, 0], ACT.Exp, scale=-1.0).then_inc(small_act, 1)
            act.wait_ge(vecs_ready, 1)
            wcols = vecs[:, 0:4 * NC].rearrange("p (l k c) -> p l k c", l=LAYERS, k=2)[:, :, 0, :]
            act.activation(edecay[:, :, :], wcols, ACT.Exp).then_inc(small_act, 1)
            act.wait_ge(small_act, 2)
            act.activation(edecay[:, :, :], edecay[:, :, :], ACT.Exp, scale=-1.0).then_inc(small_act, 1)

            def exps_F(b):
                act.wait_ge(FT_psum, b + 1)
                act.activation(kv[:, b, :, 1, :], chunked(F_bank[b]), ACT.Exp).then_inc(ek_exp, 1)
                act.activation(FT[:, b], chunked(F_bank[b]), ACT.Copy).then_inc(FT_ready, 1)

            def exps_uF(l, b):
                act.wait_ge(FT_ready, b + 1)
                if l:
                    act.wait_ge(num_ready, nth(l - 1, b) + 1)
                for c in range(NC):
                    at = NC * (2 * l + 1) + c
                    act.activation(euk[:, b, c], FT[:, b, c], ACT.Exp, bias=vecs[:, at:at + 1]).then_inc(euk_ready, 1)

            def scale(l, b):
                act.wait_ge(decay_ready, 4)
                for c in range(NC):
                    act.wait_ge(fwd_done, 2 * NC * nth(l, b) + 2 * (c + 1))
                    part = scan1[:, b, c, :, 0:T - 1]
                    act.activation(part, part, ACT.Copy, scale=one_less_d2[:, l, c, b:b + 1]).then_inc(scaled, 1)

            def reciprocal(l, b):
                act.wait_ge(den_ready, nth(l, b) + 1)
                rec = scan1[:, b, :, 0, :]
                act.activation(rec, nd[l][:, b, :, 1, :], ACT.Ln).then_inc(ln_done, 1)
                act.wait_ge(ln_done, nth(l, b) + 1)
                act.activation(rec, rec, ACT.Exp, scale=-1.0).then_inc(rec_ready, 1)

            def sigmoids(b):
                act.wait_ge(xT_psum, b + 1)
                act.activation(sig[:, b], chunked(x_bank[b]), ACT.Sigmoid).then_inc(sig_ready, 1)

            def gate_exp(i):
                act.wait_ge(negmax_ready, i + 1)
                act.activation(gexp[:, i], logits[:, i], ACT.Exp, bias=negmax[:, i:i + 1], accum_out=gsum[:, i:i + 1]).then_inc(gsum_ready, 1)

            def evacuate_hmT(i):
                act.wait_ge(hmT_psum, i + 1)
                if i >= 2:
                    act.wait_ge(y_psum, i - 1)
                act.activation(hmT[:, i % 2].rearrange("p m n -> p (m n)"), bank[HMT_BANK + i % 2][:, :], ACT.Copy).then_inc(hmT_ready, 1)

            def weights_l0():
                act.wait_ge(Wg_psum, 1)
                act.activation(WgT[:, :, :].rearrange("p c e -> p (c e)"), bank[MISC_BANK][:, WG_AT:WG_AT + NC * NE], ACT.Copy).then_inc(WgT_ready, 1)
                for c in range(NC):
                    act.wait_ge(A_psum, c + 1)
                    act.activation(AT[:, c], bank[A_bank[c]][:, :], ACT.Copy).then_inc(AT_ready, 1)
                for k in range(2):
                    act.wait_ge(B_psum, k + 1)
                    act.activation(BT[:, 2 * k:2 * k + 2].rearrange("p m o -> p (m o)"), bank[B_bank[k]][:, :], ACT.Copy,
                                   scale=EXTRA_SCALE).then_inc(BT_ready, 1)

            def abs_sum(k):
                act.wait_ge(w_loaded[k], 16)
                flat = (w1_nat if k == 0 else w2_nat)[:, :, :].rearrange("p a b -> p (a b)")
                act.activation(h32[:, :, :].rearrange("p f t -> p (f t)"), flat, ACT.Abs, accum_out=wsum[:, k:k + 1]).then_inc(wsum_ready, 1)

            def evacuate_wT(k):
                which, n = divmod(k, 2)
                act.wait_ge(qT_psum, k + 1)
                dst = w1T[:, n] if which == 0 else w2T[:, 4 * n:4 * n + 4].rearrange("p f d -> p (f d)")
                act.activation(dst, bank[WT_BANK][:, :].bitcast(BF16), ACT.Copy).then_inc(wT_ready, 1)

            exps_F(0)
            exps_uF(0, 0)
            exps_F(1)
            scale(0, 0)
            for b in range(NB):
                sigmoids(b)
            exps_F(2)
            reciprocal(0, 0)
            exps_uF(0, 1)
            exps_F(3)
            weights_l0()
            scale(0, 1)
            exps_uF(0, 2)
            reciprocal(0, 1)
            abs_sum(0)
            gate_exp(0)
            gate_exp(1)
            evacuate_hmT(0)
            scale(0, 2)
            exps_uF(0, 3)
            reciprocal(0, 2)
            abs_sum(1)
            evacuate_hmT(1)
            gate_exp(2)
            gate_exp(3)
            evacuate_hmT(2)
            scale(0, 3)
            exps_uF(1, 0)
            reciprocal(0, 3)
            evacuate_hmT(3)
            gate_exp(4)
            gate_exp(5)
            evacuate_hmT(4)
            evacuate_wT(0)
            evacuate_wT(1)
            scale(1, 0)
            exps_uF(1, 1)
            reciprocal(1, 0)
            evacuate_hmT(5)
            gate_exp(6)
            gate_exp(7)
            evacuate_hmT(6)
            evacuate_wT(2)
            scale(1, 1)
            exps_uF(1, 2)
            reciprocal(1, 1)
            evacuate_hmT(7)
            evacuate_wT(3)

            def tanh(b):
                act.wait_ge(x1T_psum, b + 1)
                act.wait_ge(cond_ready, b + 1)
                act.activation(sig[:, b], chunked(x1T_bank[b % 2]), ACT.Tanh, scale=0.5).then_inc(tanh_ready, 1)

            def xin_high(b):
                act.wait_ge(xin_ready, b + 1)
                if b >= 2:
                    act.wait_ge(g_psum, NJ * (b - 1))
                act.activation(xin_hi[:, b % 2], sig[:, b], ACT.Copy, scale=out_scale[:, 1, b:b + 1]).then_inc(xhi_ready, 1)

            def gelus(b):
                for j in range(NJ):
                    act.wait_ge(g_psum, NJ * b + j + 1)
                    if b:
                        act.wait_ge(hlo_ready, NJ * (b - 1) + j + 1)
                    for f in (2 * j, 2 * j + 1):
                        act.activation(h32[:, f], bank[j][:, (f % 2) * T:(f % 2 + 1) * T], ACT.Gelu,
                                       bias=vecs[:, 4 * NC + f:4 * NC + f + 1]).then_inc(h32_ready, 1)
                    act.wait_ge(h32_ready, NF * b + 2 * j + 2)
                    if b >= 2:
                        act.wait_ge(o_psum, NT * (b - 1))
                    act.activation(h_hi[:, b % 2, 2 * j:2 * j + 2], h32[:, 2 * j:2 * j + 2], ACT.Copy).then_inc(hhi_ready, 1)

            scale(1, 2)
            exps_uF(1, 3)
            reciprocal(1, 2)
            scale(1, 3)
            reciprocal(1, 3)
            tanh(0)
            tanh(1)
            xin_high(0)
            for b in range(NB):
                if b + 1 < NB:
                    if b + 1 >= 2:
                        tanh(b + 1)
                    xin_high(b + 1)
                gelus(b)

        @block.vector
        def _(dve):
            dve.wait_ge(cond_loaded, 16)
            dve.tensor_reduce(tf[:, 0], cond_all[:, :, :], AX_X, ALU.add).then_inc(small_dve, 1)
            dve.wait_ge(consts_ready, 2)
            dve.tensor_copy(identb[:, :], ident[:, :]).then_inc(identb_ready, 1)
            dve.wait_ge(vec_psum, 1)
            dve.tensor_copy(vecs[:, :], bank[MISC_BANK][:, VEC_AT:VEC_AT + NV]).then_inc(vecs_ready, 1)
            dve.wait_ge(small_act, 1)
            dve.tensor_scalar(tf[:, 1], tf[:, 1], 1.0, None, ALU.add).then_inc(small_dve, 1)
            dve.wait_ge(small_dve, 2)
            dve.reciprocal(tf[:, 2], tf[:, 1]).then_inc(small_dve, 1)
            dve.wait_ge(small_dve, 3)
            dve.tensor_scalar(out_scale[:, 0], tf[:, 2], -0.2, -0.8, ALU.mult, ALU.add).then_inc(small_dve, 1)
            dve.tensor_scalar(out_scale[:, 1], tf[:, 2], -0.1, -0.4, ALU.mult, ALU.add).then_inc(small_dve, 1)
            dve.tensor_scalar(tf[:, 0], tf[:, 2], 0.5, 0.5, ALU.mult, ALU.add).then_inc(small_dve, 1)
            dve.wait_ge(small_dve, 6)
            dve.wait_ge(small_act, 3)
            for l in range(LAYERS):
                for c in range(NC):
                    dve.tensor_scalar(decay[:, l, c], tf[:, 0], edecay[:, l, c:c + 1], None, ALU.mult).then_inc(small_dve, 1)
            dve.wait_ge(small_dve, 10)
            flat = "p l c b -> p (l c b)"
            dve.scalar_tensor_tensor(one_less_d2[:, :, :, :].rearrange(flat), decay[:, :, :, :].rearrange(flat), -1.0,
                                     decay[:, :, :, :].rearrange(flat), ALU.mult, ALU.mult).then_inc(decay_ready, 3)
            dve.wait_ge(decay_ready, 3)
            dve.tensor_scalar(one_less_d2[:, :, :, :].rearrange(flat), one_less_d2[:, :, :, :].rearrange(flat), 1.0, None,
                              ALU.add).then_inc(decay_ready, 1)

            def keys_values(b):
                dve.wait_ge(ek_exp, b + 1)
                dve.wait_ge(FT_ready, b + 1)
                dve.scalar_tensor_tensor(kv[:, b, :, 0, :], kv[:, b, :, 1, :], EXP30, FT[:, b], ALU.min,
                                         ALU.mult).then_inc(ekv_ready, 1)
                dve.wait_ge(ekv_ready, b + 1)
                dve.tensor_scalar(kv[:, b, :, 1, :], kv[:, b, :, 1, :], EXP30, None, ALU.min).then_inc(kv_ready, 1)

            def forward(l, b):
                dve.wait_ge(kv_ready, b + 1)
                if l:
                    dve.wait_ge(ratio_ready, nth(l - 1, b) + 1)
                for c in range(NC):
                    for q in range(2):
                        dve.tensor_tensor_scan(scan1[:, b, c, q], decay[:, l, c, b:b + 1].broadcast_to([P, T]), kv[:, b, c, q],
                                               0.0, ALU.mult, ALU.add).then_inc(fwd_done, 1)

            def backward(l, b):
                for c in range(NC):
                    dve.wait_ge(scaled, NC * nth(l, b) + c + 1)
                    for q in (1, 0):
                        dve.tensor_tensor_scan(nd[l][:, b, c, q, ::-1], decay[:, l, c, b:b + 1].broadcast_to([P, T]),
                                               scan1[:, b, c, q, ::-1], 0.0, ALU.mult, ALU.add).then_inc(bwd_done, 1)

            def denominators(l, b):
                dve.wait_ge(euk_ready, NC * nth(l, b) + NC)
                dve.wait_ge(bwd_done, 2 * NC * nth(l, b) + 2 * NC)
                den = nd[l][:, b, :, 1, :]
                dve.scalar_tensor_tensor(den, euk[:, b], EXP30, den, ALU.min, ALU.add).then_inc(den_ready, 1)
                dve.scalar_tensor_tensor(euk[:, b], euk[:, b], EXP30, FT[:, b], ALU.min, ALU.mult).then_inc(eukv_ready, 1)

            def ratio(l, b):
                dve.wait_ge(dr_ready, nth(l, b) + 1)
                dve.wait_ge(q_ready, nth(l, b) + 1)
                num = nd[l][:, b, :, 0, :]
                dve.scalar_tensor_tensor(num, scan1[:, b, :, 1, :], 2.0, num, ALU.subtract, ALU.mult).then_inc(ratio_ready, 1)
                if l == 0:
                    dve.wait_ge(ratio_ready, nth(l, b) + 1)
                    dve.wait_ge(sig_ready, b + 1)
                    dve.scalar_tensor_tensor(num, num, out_scale[:, 0, b:b + 1], sig[:, b], ALU.mult, ALU.mult).then_inc(cond_ready, 1)

            def gate(i):
                lg = logits[:, i]
                dve.wait_ge(logits_psum, i + 1)
                dve.tensor_copy(lg, bank[MISC_BANK][:, LOGIT_AT:LOGIT_AT + NE]).then_inc(logits_ready, 1)
                dve.wait_ge(logits_ready, i + 1)
                dve.max(mx8[:, i], lg).then_inc(max_ready, 1)
                dve.wait_ge(max_ready, i + 1)
                dve.tensor_scalar(negmax[:, i:i + 1], mx8[:, i, 0:1], -1.0, None, ALU.mult).then_inc(negmax_ready, 1)
                dve.max_index(idx8[:, i], mx8[:, i], lg).then_inc(idx_ready, 1)
                dve.wait_ge(idx_ready, i + 1)
                dve.wait_ge(consts_ready, 3 + NE)
                dve.tensor_scalar(mask[:, i], iota8[:, :], idx8[:, i, 0:1], None, ALU.is_equal).then_inc(mask_ready, 1)

            def select_expert(i):
                dve.wait_ge(gsum_ready, i + 1)
                dve.reciprocal(grec[:, i:i + 1], gsum[:, i:i + 1]).then_inc(grec_ready, 1)
                dve.wait_ge(grec_ready, i + 1)
                dve.wait_ge(mask_ready, i + 1)
                dve.wait_ge(h_psum, i + 1)
                if i >= 2:
                    dve.wait_ge(hmT_psum, i - 1)
                dve.scalar_tensor_tensor(hm[:, i % 2].rearrange("p (e r) -> p e r", e=NE),
                                         bank[H_BANK + i % 2][:, :].rearrange("p (e r) -> p e r", e=NE), grec[:, i:i + 1],
                                         mask[:, i].rearrange("p (e a) -> p e a", a=1).broadcast_to([P, NE, R]),
                                         ALU.mult, ALU.mult).then_inc(hm_ready, 1)

            def residual(i):
                dve.wait_ge(y_psum, i + 1)
                dve.wait_ge(x_loaded[i // NT], 16)
                dve.tensor_tensor(x_nat[:, i], x_nat[:, i], bank[Y_BANK + i % 2][:, 0:C], ALU.add).then_inc(x1_ready, 1)

            def thresholds(k):
                dve.wait_ge(wtot_psum, k + 1)
                tot = bank[MISC_BANK][:, WTOT_AT + k:WTOT_AT + k + 1]
                dve.tensor_scalar(thr[:, k, 0:1], tot, 1.0 / (DFF * C), 0.7, ALU.mult, ALU.mult).then_inc(thr_ready, 1)
                dve.wait_ge(thr_ready, 2 * k + 1)
                dve.tensor_scalar(thr[:, k, 1:2], thr[:, k, 0:1], -1.0, None, ALU.mult).then_inc(thr_ready, 1)

            def quantise(k):
                dve.wait_ge(neg_ready, k + 1)
                flat_w = (w1_nat if k == 0 else w2_nat)[:, :, :].rearrange("p a b -> p (a b)")
                flat_q = (q1 if k == 0 else q2)[:, :, :].rearrange("p a b -> p (a b)")
                dve.scalar_tensor_tensor(flat_q, flat_w, thr[:, k, 0:1], neg_part[:, :], ALU.is_ge, ALU.subtract).then_inc(quant_ready, 1)

            def cond_a(l, b):
                forward(l, b)
                backward(l, b)
                denominators(l, b)

            keys_values(0)
            cond_a(0, 0)
            ratio_products(dve, 0, 0)
            ratio(0, 0)
            keys_values(1)
            cond_a(0, 1)
            gate(0)
            keys_values(2)
            select_expert(0)
            gate(1)
            select_expert(1)
            forward(0, 2)
            ratio(0, 1)
            backward(0, 2)
            denominators(0, 2)
            residual(0)
            thresholds(0)
            gate(2)
            select_expert(2)
            keys_values(3)
            residual(1)
            gate(3)
            select_expert(3)
            ratio(0, 2)
            forward(0, 3)
            backward(0, 3)
            denominators(0, 3)
            residual(2)
            thresholds(1)
            gate(4)
            select_expert(4)
            residual(3)
            quantise(0)
            gate(5)
            select_expert(5)
            ratio(0, 3)
            cond_a(1, 0)
            residual(4)
            gate(6)
            select_expert(6)
            residual(5)
            gate(7)
            select_expert(7)
            quantise(1)
            ratio(1, 0)
            cond_a(1, 1)
            residual(6)
            residual(7)

            def ffn_input(b):
                dve.wait_ge(tanh_ready, b + 1)
                dve.wait_ge(ratio_ready, nth(1, b) + 1)
                dve.scalar_tensor_tensor(sig[:, b], sig[:, b], 1.0, nd[1][:, b, :, 0, :], ALU.add, ALU.mult).then_inc(xin_ready, 1)

            def xin_low(b):
                dve.wait_ge(xhi_ready, b + 1)
                if b >= 2:
                    dve.wait_ge(g_psum, NJ * (b - 1))
                dve.scalar_tensor_tensor(xin_lo[:, b % 2], sig[:, b], out_scale[:, 1, b:b + 1], xin_hi[:, b % 2].bitcast(F32),
                                         ALU.mult, ALU.subtract).then_inc(xlo_ready, 1)

            def h_low(b):
                if b >= 2:
                    dve.wait_ge(o_psum, NT * (b - 1))
                for j in range(NJ):
                    dve.wait_ge(hhi_ready, NJ * b + j + 1)
                    dve.tensor_tensor(h_lo[:, b % 2, 2 * j:2 * j + 2], h32[:, 2 * j:2 * j + 2], h_hi[:, b % 2, 2 * j:2 * j + 2].bitcast(F32),
                                      ALU.subtract).then_inc(hlo_ready, 1)

            def result(i):
                dve.wait_ge(o_psum, i + 1)
                dve.wait_ge(x1b_ready, i + 1)
                if i >= 2:
                    dve.wait_ge(out_stored[i % 2], 16 * (i // 2))
                dve.tensor_tensor(outb[:, i % 2], bank[Y_BANK + i % 2][:, 0:C], x1b[:, i], ALU.add).then_inc(out_ready, 1)

            cond_a(1, 2)
            ratio(1, 1)
            cond_a(1, 3)
            ratio(1, 2)
            ratio(1, 3)
            ffn_input(0)
            xin_low(0)
            ffn_input(1)
            for b in range(NB):
                if b + 1 < NB:
                    if b + 1 >= 2:
                        ffn_input(b + 1)
                    xin_low(b + 1)
                h_low(b)
                if b:
                    result(2 * b - 2)
                    result(2 * b - 1)
            result(NI - 2)
            result(NI - 1)

        @block.tensor
        def _(pe):
            pe.wait_ge(consts_ready, 2)
            pe.wait_ge(vec_loaded, 16 * 5)
            pe.transpose(bank[MISC_BANK][:, VEC_AT:VEC_AT + NV], vec_rows[:, :], ident[0:NV, 0:NV]).then_inc(vec_psum, 1)

            def transpose_F(b):
                pe.wait_ge(F_loaded[b], 16)
                if b == 3:
                    pe.wait_ge(FT_ready, 1)
                for c in range(NC):
                    for n in range(NT):
                        mm = pe.transpose(bank[F_bank[b]][:, c * T + n * P:c * T + (n + 1) * P],
                                          F_nat[:, b, n, c * P:(c + 1) * P], ident[:, :])
                mm.then_inc(FT_psum, 1)

            def transpose_x(b):
                pe.wait_ge(x_loaded[b], 16)
                for c in range(NC):
                    for n in range(NT):
                        mm = pe.transpose(bank[x_bank[b]][:, c * T + n * P:c * T + (n + 1) * P],
                                          x_nat[:, NT * b + n, c * P:(c + 1) * P], ident[:, :])
                mm.then_inc(xT_psum, 1)

            transpose_F(0)
            transpose_F(1)
            for b in range(NB):
                transpose_x(b)
            transpose_F(2)
            pe.wait_ge(Wg_loaded, 16)
            pe.wait_ge(vecs_ready, 1)
            for c in range(NC):
                mm = pe.transpose(bank[MISC_BANK][:, WG_AT + NE * c:WG_AT + NE * (c + 1)], Wg_nat[:, c * P:(c + 1) * P], ident[0:NE, 0:NE])
            mm.then_inc(Wg_psum, 1)
            transpose_F(3)
            pe.wait_ge(A_loaded, 16)
            for c in range(NC):
                if c == 0:
                    pe.wait_ge(FT_ready, 2)
                else:
                    pe.wait_ge(sig_ready, 1)
                for m in range(NM):
                    mm = pe.transpose(bank[A_bank[c]][:, m * P:(m + 1) * P], A_nat[:, m, c * P:(c + 1) * P], ident[:, :])
                mm.then_inc(A_psum, 1)
            pe.wait_ge(B_loaded, 16 * NC)
            for k in range(2):
                pe.wait_ge(sig_ready, k + 2)
                for m in (2 * k, 2 * k + 1):
                    for o in range(NC):
                        at = (m % 2) * C + o * P
                        mm = pe.transpose(bank[B_bank[k]][:, at:at + P], B_nat[:, o].rearrange("p e r -> p (e r)")[:, m * P:(m + 1) * P], ident[:, :])
                mm.then_inc(B_psum, 1)

            def logits_and_h(i):
                b, n = divmod(i, NT)
                xc = [nd[0][:, b, c, 0, n * P:(n + 1) * P] for c in range(NC)]
                pe.wait_ge(cond_ready, b + 1)
                if i == 0:
                    pe.wait_ge(WgT_ready, 1)
                lg = bank[MISC_BANK][:, LOGIT_AT:LOGIT_AT + NE]
                if i:
                    pe.wait_ge(logits_ready, i)
                if i in TOTAL_AT:
                    pe.wait_ge(thr_ready, 2 * TOTAL_AT.index(i) + 1)
                for c in range(NC):
                    mm = pe.matmul(lg, xc[c], WgT[:, c], start=(c == 0), stop=(c == NC - 1))
                mm.then_inc(logits_psum, 1)
                if i == 0:
                    pe.wait_ge(AT_ready, NC)
                    pe.wait_ge(BT_ready, 1)
                if i >= 2:
                    pe.wait_ge(hm_ready, i - 1)
                for c in range(NC):
                    mm = pe.matmul(bank[H_BANK + i % 2][:, :], xc[c], AT[:, c], start=(c == 0), stop=(c == NC - 1))
                mm.then_inc(h_psum, 1)

            def transpose_hm(i):
                pe.wait_ge(hm_ready, i + 1)
                if i == 0:
                    pe.wait_ge(FT_ready, NB)
                if i >= 2:
                    pe.wait_ge(hmT_ready, i - 1)
                for m in range(NM):
                    mm = pe.transpose(bank[HMT_BANK + i % 2][:, m * P:(m + 1) * P], hm[:, i % 2, m * P:(m + 1) * P], ident[:, :])
                mm.then_inc(hmT_psum, 1)

            def expert_out(i):
                pe.wait_ge(hmT_ready, i + 1)
                if i == 0:
                    pe.wait_ge(BT_ready, 2)
                if i == 1:
                    pe.wait_ge(sig_ready, NB)
                if i >= 2:
                    pe.wait_ge(x1_ready, i - 1)
                for m in range(NM):
                    mm = pe.matmul(bank[Y_BANK + i % 2][:, 0:C], hmT[:, i % 2, m], BT[:, m],
                                   start=(m == 0), stop=(m == NM - 1))
                mm.then_inc(y_psum, 1)

            def weight_total(k):
                pe.wait_ge(wsum_ready, k + 1)
                pe.wait_ge(logits_ready, TOTAL_AT[k])
                pe.wait_ge(consts_ready, 3)
                pe.matmul(bank[MISC_BANK][:, WTOT_AT + k:WTOT_AT + k + 1], ones[:, :], wsum[:, k:k + 1],
                          start=True, stop=True).then_inc(wtot_psum, 1)

            def transpose_weights(k):
                which, n = divmod(k, 2)
                pe.wait_ge(quant_ready, which + 1)
                pe.wait_ge(identb_ready, 1)
                if k == 0:
                    pe.wait_ge(FT_ready, 3)
                else:
                    pe.wait_ge(wT_ready, k)
                for s in range(8):
                    if which == 0:
                        src = q1[:, s, n * P:(n + 1) * P]
                    else:
                        f = 4 * n + s // 2
                        src = q2[:, s % 2, f * P:(f + 1) * P]
                    mm = pe.transpose(bank[WT_BANK][:, :].bitcast(BF16)[:, s * P:(s + 1) * P], src, identb[:, :])
                mm.then_inc(qT_psum, 1)

            for i in range(NI + 1):
                if i < NI:
                    logits_and_h(i)
                if i >= 1:
                    transpose_hm(i - 1)
                    expert_out(i - 1)
                if i + 1 in TOTAL_AT:
                    weight_total(TOTAL_AT.index(i + 1))
                if i in WT_AT:
                    transpose_weights(WT_AT.index(i))

            def transpose_x1(b):
                pe.wait_ge(x1_ready, NT * (b + 1))
                if b < 2:
                    pe.wait_ge(wT_ready, 4)
                else:
                    pe.wait_ge(tanh_ready, b - 1)
                for c in range(NC):
                    for n in range(NT):
                        mm = pe.transpose(bank[x1T_bank[b % 2]][:, c * T + n * P:c * T + (n + 1) * P],
                                          x_nat[:, NT * b + n, c * P:(c + 1) * P], ident[:, :])
                mm.then_inc(x1T_psum, 1)

            def hidden(b):
                pe.wait_ge(xlo_ready, b + 1)
                for j in range(NJ):
                    if b:
                        pe.wait_ge(h32_ready, NF * (b - 1) + 2 * j + 2)
                    for f in (2 * j, 2 * j + 1):
                        for c in range(NC):
                            for part in (xin_hi, xin_lo):
                                mm = pe.matmul(bank[j][:, (f % 2) * T:(f % 2 + 1) * T], w1T[:, c, f * P:(f + 1) * P],
                                               part[:, b % 2, c], start=(c == 0 and part is xin_hi),
                                               stop=(c == NC - 1 and part is xin_lo))
                    mm.then_inc(g_psum, 1)

            def ffn_out(b):
                for n in range(NT):
                    i = NT * b + n
                    if i >= 2:
                        pe.wait_ge(out_ready, i - 1)
                    for f in range(NF):
                        pe.wait_ge(hlo_ready, NJ * b + f // 2 + 1)
                        for part in (h_hi, h_lo):
                            mm = pe.matmul(bank[Y_BANK + n][:, 0:C], part[:, b % 2, f, n * P:(n + 1) * P], w2T[:, f],
                                           start=(f == 0 and part is h_hi), stop=(f == NF - 1 and part is h_lo))
                    mm.then_inc(o_psum, 1)

            transpose_x1(0)
            transpose_x1(1)
            for b in range(NB):
                if 2 <= b + 1 < NB:
                    transpose_x1(b + 1)
                hidden(b)
                if b:
                    ffn_out(b - 1)
            ffn_out(NB - 1)


_INS = ['x', 'fside_BxSxS_0', 'cond_512', 'L0_cond_w', 'L0_cond_u', 'L0_ffn_A', 'L0_ffn_Bw', 'L0_ffn_Wg',
        'L1_cond_w', 'L1_cond_u', 'L1_ffn_w1', 'L1_ffn_b1', 'L1_ffn_w2', 'L1_ffn_b2']
_OUTS = [((4, 256, 256), 'float32')]


def kernel(**inputs):
    import numpy as _np
    import concourse.bacc as _bacc
    from concourse import mybir as _mybir
    from concourse.bass_utils import run_bass_kernel_spmd as _run

    nc = _bacc.Bacc("TRN2", target_bir_lowering=False, num_devices=1)
    arrays, args = {}, []
    for name in _INS:
        a = _np.ascontiguousarray(inputs[name])
        arrays[f"in_{name}_dram"] = a
        args.append(nc.dram_tensor(f"in_{name}_dram", a.shape, _mybir.dt.from_np(a.dtype), kind="ExternalInput").ap())
    for i, (shape, dtype) in enumerate(_OUTS):
        dt = _mybir.dt.from_np(_np.dtype(dtype))
        args.append(nc.dram_tensor(f"out_{i}_dram", shape, dt, kind="ExternalOutput").ap())
    adaln_ffn_kernel(nc, *args)
    r = _run(nc, [arrays], core_ids=[0])
    return r.results[0]["out_0_dram"]
```

```python
from contextlib import ExitStack

import concourse.bass as bass
from concourse import mybir

ALU = mybir.AluOpType
ACT = mybir.ActivationFunctionType
F32 = mybir.dt.float32
F32R = mybir.dt.float32r
BF16 = mybir.dt.bfloat16
U32 = mybir.dt.uint32
AX_X = mybir.AxisListType.X

P = 128
EXP30 = 1.0686474581524463e13


def adaln_ffn_kernel(nc, x, fside, cond, w_l0, u_l0, A, Bw, Wg, w_l1, u_l1, w1, b1, w2, b2, out):
    NB, T, C = x.shape
    NE, R, _ = A.shape
    DFF = w1.shape[0]
    TD = cond.shape[1]
    NC = C // P
    NT = T // P
    NI = NB * NT
    ER = NE * R
    NM = ER // P
    NF = DFF // P
    NJ = NF // 2
    NV = 4 * NC + NF
    LAYERS = 2
    EXTRA_SCALE = 4.0
    assert NC == 2 and NT == 2 and ER == 512 and NF == 8 and NB == 4

    with ExitStack() as ctx:
        def sb(name, shape, dt=F32, where=ctx):
            return where.enter_context(nc.sbuf_tensor(name, shape, dt))

        def sem(name):
            return ctx.enter_context(nc.semaphore(name))

        bank = [ctx.enter_context(nc.psum_tensor(f"bank{k}", [P, 512], F32)) for k in range(8)]

        ident = sb("ident", [P, P])
        identb = sb("identb", [P, P], BF16)
        ones = sb("ones", [P, P])
        iota8 = sb("iota8", [P, NE])
        vec_rows = sb("vec_rows", [NV, P])
        vecs = sb("vecs", [P, NV])
        cond_all = sb("cond_all", [P, NB, TD])
        tf = sb("tf", [P, 3, NB])
        out_scale = sb("out_scale", [P, 2, NB])
        edecay = sb("edecay", [P, LAYERS, NC])
        decay = sb("decay", [P, LAYERS, NC, NB])
        one_less_d2 = sb("one_less_d2", [P, LAYERS, NC, NB])
        b2_all = sb("b2_all", [P, C])
        x_nat = sb("x_nat", [P, NI, C])
        x1b = sb("x1b", [P, NI, C])
        FT = sb("FT", [P, NB, NC, T])
        kv = sb("kv", [P, NB, NC, 2, T])
        euk = sb("euk", [P, NB, NC, T])
        scan1 = sb("scan1", [P, NB, NC, 2, T])
        nd = [sb(f"nd{l}", [P, NB, NC, 2, T]) for l in range(LAYERS)]
        sig = sb("sig", [P, NB, NC, T])
        xin_hi = sb("xin_hi", [P, 2, NC, T], F32R)
        xin_lo = sb("xin_lo", [P, 2, NC, T], F32R)
        WgT = sb("WgT", [P, NC, NE])
        AT = sb("AT", [P, NC, ER])
        BT = sb("BT", [P, NM, C])
        w1T = sb("w1T", [P, NC, DFF], F32R)
        w2T = sb("w2T", [P, NF, C], F32R)
        q1 = sb("q1", [P, NF, C], BF16)
        q2 = sb("q2", [P, NC, DFF], BF16)
        wsum = sb("wsum", [P, 2])
        thr = sb("thr", [P, 2, 2])
        mx8 = sb("mx8", [P, NI, NE])
        idx8 = sb("idx8", [P, NI, NE], U32)
        negmax = sb("negmax", [P, NI])
        logits = sb("logits", [P, NI, NE])
        gexp = sb("gexp", [P, NI, NE])
        gsum = sb("gsum", [P, NI])
        grec = sb("grec", [P, NI])
        mask = sb("mask", [P, NI, NE])
        hm = sb("hm", [P, 2, ER])
        hmT = sb("hmT", [P, 2, NM, P])
        h32 = sb("h32", [P, NF, T])
        outb = sb("outb", [P, 2, C])
        early = ExitStack()
        F_nat = sb("F_nat", [P, NB, NT, C], F32, early)
        w1_nat = sb("w1_nat", [P, NF, C], F32, early)
        w2_nat = sb("w2_nat", [P, NC, DFF], F32, early)
        A_nat = sb("A_nat", [P, NM, C], F32, early)
        B_nat = sb("B_nat", [P, NC, NE, R], F32, early)
        Wg_nat = sb("Wg_nat", [NE, C], F32, early)
        neg_part = sb("neg_part", [P, 2 * DFF], BF16, early)
        early.close()
        h_hi = sb("h_hi", [P, 2, NF, T], F32R)
        h_lo = sb("h_lo", [P, 2, NF, T], F32R)

        def per(kind, n):
            return [sem(f"{kind}_{k}") for k in range(n)]

        F_loaded, x_loaded = per("F_loaded", NB), per("x_loaded", NB)
        vec_loaded, cond_loaded, b2_loaded = sem("vec_loaded"), sem("cond_loaded"), sem("b2_loaded")
        Wg_loaded, A_loaded, B_loaded = sem("Wg_loaded"), sem("A_loaded"), sem("B_loaded")
        w_loaded = per("w_loaded", 2)
        consts_ready, identb_ready = sem("consts_ready"), sem("identb_ready")
        FT_psum, xT_psum = sem("FT_psum"), sem("xT_psum")
        vec_psum, vecs_ready = sem("vec_psum"), sem("vecs_ready")
        small_dve, small_act, decay_ready = sem("small_dve"), sem("small_act"), sem("decay_ready")
        ek_exp, ekv_ready, kv_ready = sem("ek_exp"), sem("ekv_ready"), sem("kv_ready")
        ek_ready = sem("ek_ready")
        FT_ready, sig_ready = sem("FT_ready"), sem("sig_ready")
        euk_ready = per("euk_ready", LAYERS)
        fwd_done, scaled, bwd_done = per("fwd_done", LAYERS), per("scaled", LAYERS), per("bwd_done", LAYERS)
        clip_ready = per("clip_ready", LAYERS)
        den_ready, eukv_ready, num_ready = per("den_ready", LAYERS), per("eukv_ready", LAYERS), per("num_ready", LAYERS)
        ln_done, rec_ready = per("ln_done", LAYERS), per("rec_ready", LAYERS)
        dr_ready, q_ready, ratio_ready = per("dr_ready", LAYERS), per("q_ready", LAYERS), per("ratio_ready", LAYERS)
        cond_ready = sem("cond_ready")
        Wg_psum, A_psum, B_psum = sem("Wg_psum"), sem("A_psum"), sem("B_psum")
        WgT_ready, AT_ready, BT_ready = sem("WgT_ready"), sem("AT_ready"), sem("BT_ready")
        wsum_ready, wtot_psum, thr_ready = sem("wsum_ready"), sem("wtot_psum"), sem("thr_ready")
        neg_ready, quant_ready = sem("neg_ready"), sem("quant_ready")
        qT_psum, wT_ready = sem("qT_psum"), sem("wT_ready")
        logits_ready = sem("logits_ready")
        logits_psum, h_psum = sem("logits_psum"), sem("h_psum")
        max_ready, negmax_ready, idx_ready = sem("max_ready"), sem("negmax_ready"), sem("idx_ready")
        mask_ready, gsum_ready, grec_ready = sem("mask_ready"), sem("gsum_ready"), sem("grec_ready")
        hm_ready, hmT_psum, hmT_ready = sem("hm_ready"), sem("hmT_psum"), sem("hmT_ready")
        y_psum, x1_ready, x1b_ready = sem("y_psum"), sem("x1_ready"), sem("x1b_ready")
        x1T_psum, tanh_ready, xin_ready = sem("x1T_psum"), sem("tanh_ready"), sem("xin_ready")
        xhi_ready, xlo_ready = sem("xhi_ready"), sem("xlo_ready")
        g_psum, h32_ready, hhi_ready, hlo_ready = sem("g_psum"), sem("h32_ready"), sem("hhi_ready"), sem("hlo_ready")
        o_psum, out_ready = sem("o_psum"), sem("out_ready")
        out_stored = per("out_stored", 2)

        F_bank = [0, 1, 7, 0]
        x_bank = [2, 3, 4, 5]
        A_bank, B_bank = [1, 2], [3, 4]
        WT_BANK = 7
        x1T_bank = [6, 7]
        HMT_BANK, H_BANK, Y_BANK, MISC_BANK = 0, 2, 4, 6
        VEC_AT, WG_AT, LOGIT_AT = 0, 32, 128

        def chunked(k):
            return bank[k][:, :].rearrange("p (c t) -> p c t", c=NC)

        def in_turn(eng, done, l, b):
            if b and l == 0:
                eng.wait_ge(done[0], b)

        def clip_euk(eng, l, b):
            eng.wait_ge(euk_ready[l], NC * b + NC)
            in_turn(eng, clip_ready, l, b)
            eng.tensor_scalar(euk[:, b], euk[:, b], EXP30, 0.0, ALU.min, ALU.max).then_inc(clip_ready[l], 1)

        def times_v(eng, l, b):
            eng.wait_ge(den_ready[l], b + 1)
            in_turn(eng, eukv_ready, l, b)
            eng.tensor_tensor(euk[:, b], euk[:, b], FT[:, b], ALU.mult).then_inc(eukv_ready[l], 1)

        def add_num(eng, l, b):
            num = nd[l][:, b, :, 0, :]
            eng.wait_ge(bwd_done[l], 2 * NC * (b + 1))
            eng.wait_ge(eukv_ready[l], b + 1)
            in_turn(eng, num_ready, l, b)
            eng.tensor_tensor(num, num, euk[:, b], ALU.add).then_inc(num_ready[l], 1)

        def den_times_rec(eng, l, b):
            eng.wait_ge(rec_ready[l], b + 1)
            in_turn(eng, dr_ready, l, b)
            eng.tensor_tensor(scan1[:, b, :, 1, :], nd[l][:, b, :, 1, :], scan1[:, b, :, 0, :], ALU.mult).then_inc(dr_ready[l], 1)

        def num_times_rec(eng, l, b):
            num = nd[l][:, b, :, 0, :]
            eng.wait_ge(rec_ready[l], b + 1)
            eng.wait_ge(num_ready[l], b + 1)
            in_turn(eng, q_ready, l, b)
            eng.tensor_tensor(num, num, scan1[:, b, :, 0, :], ALU.mult).then_inc(q_ready[l], 1)

        block = ctx.enter_context(nc.Block())

        @block.sync
        def _(sp):
            F_tiles = fside.rearrange("b (n p) c -> b p n c", p=P)
            x_tiles = x.rearrange("b (n p) c -> b p n c", p=P)
            sp.dma_start(F_nat[:, 0], F_tiles[0]).then_inc(F_loaded[0], 16)
            for k, v in enumerate((w_l0, u_l0)):
                sp.dma_start(vec_rows[NC * k:NC * (k + 1), :], v.rearrange("(c p) -> c p", p=P)).then_inc(vec_loaded, 16)
            for b in range(NB):
                sp.dma_start(x_nat[:, NT * b:NT * (b + 1)], x_tiles[b]).then_inc(x_loaded[b], 16)
                if b + 1 < NB:
                    sp.dma_start(F_nat[:, b + 1], F_tiles[b + 1]).then_inc(F_loaded[b + 1], 16)
            sp.dma_start(A_nat[:, :, :], A.rearrange("e r c -> (e r) c").rearrange("(m p) c -> p m c", p=P)).then_inc(A_loaded, 16)
            for c in range(NC):
                sp.dma_start(B_nat[:, c], Bw[:, c * P:(c + 1) * P, :].rearrange("e o r -> o e r")).then_inc(B_loaded, 16)
            sp.dma_start(w1_nat[:, :, :], w1.rearrange("(n p) c -> p n c", p=P)).then_inc(w_loaded[0], 16)
            sp.dma_start(w2_nat[:, :, :], w2.rearrange("(n p) f -> p n f", p=P)).then_inc(w_loaded[1], 16)
            sp.dma_start(b2_all[:, :], b2.rearrange("(a n) -> a n", a=1).broadcast_to([P, C])).then_inc(b2_loaded, 16)
            out_tiles = out.rearrange("b (n p) c -> (b n) p c", p=P)
            for i in range(NI):
                sp.wait_ge(out_ready, i + 1)
                sp.dma_start(out_tiles[i], outb[:, i % 2]).then_inc(out_stored[i % 2], 16)
            for k in range(2):
                sp.wait_ge(out_stored[k], 16 * NI // 2)

        @block.gpsimd
        def _(pool):
            pool.memset(ident[:, :], 0.0).then_inc(consts_ready, 1)
            pool.wait_ge(consts_ready, 1)
            pool.affine_select(out=ident[:, :], in_=ident[:, :], compare_op=ALU.not_equal, fill=1.0, base=0,
                               pattern=[[-1, P]], channel_multiplier=1).then_inc(consts_ready, 1)
            pool.memset(ones[:, :], 1.0).then_inc(consts_ready, 1)
            for e in range(NE):
                pool.memset(iota8[:, e:e + 1], float(e)).then_inc(consts_ready, 1)

            def pool_keys_values(b):
                pool.wait_ge(FT_ready, b + 1)
                pool.wait_ge(kv_ready, b)
                pool.tensor_scalar(kv[:, b, :, 1, :], kv[:, b, :, 1, :], EXP30, 0.0, ALU.min, ALU.max).then_inc(ek_ready, 1)
                pool.wait_ge(ek_ready, b)
                pool.tensor_tensor(kv[:, b, :, 0, :], kv[:, b, :, 1, :], FT[:, b], ALU.mult).then_inc(kv_ready, 1)

            def add_b2(i):
                pool.wait_ge(b2_loaded, 16)
                pool.wait_ge(x1_ready, i + 1)
                pool.tensor_tensor(x1b[:, i], x_nat[:, i], b2_all[:, :], ALU.add).then_inc(x1b_ready, 1)

            pool_keys_values(1)
            clip_euk(pool, 0, 1)
            pool_keys_values(2)
            pool_keys_values(3)
            times_v(pool, 0, 1)
            clip_euk(pool, 0, 2)
            add_num(pool, 0, 1)
            den_times_rec(pool, 0, 1)
            num_times_rec(pool, 0, 1)
            times_v(pool, 0, 2)
            add_num(pool, 0, 2)
            clip_euk(pool, 0, 3)
            num_times_rec(pool, 0, 2)
            den_times_rec(pool, 0, 2)
            clip_euk(pool, 1, 0)
            clip_euk(pool, 1, 1)
            times_v(pool, 0, 3)
            clip_euk(pool, 1, 2)
            add_num(pool, 0, 3)
            den_times_rec(pool, 0, 3)
            num_times_rec(pool, 0, 3)
            clip_euk(pool, 1, 3)
            add_b2(0)
            add_b2(1)
            times_v(pool, 1, 0)
            den_times_rec(pool, 1, 0)
            add_num(pool, 1, 0)
            add_b2(2)
            num_times_rec(pool, 1, 0)
            add_b2(3)
            times_v(pool, 1, 1)
            add_num(pool, 1, 1)
            den_times_rec(pool, 1, 1)
            num_times_rec(pool, 1, 1)
            times_v(pool, 1, 2)
            den_times_rec(pool, 1, 2)
            add_num(pool, 1, 2)
            times_v(pool, 1, 3)
            num_times_rec(pool, 1, 2)
            add_num(pool, 1, 3)
            den_times_rec(pool, 1, 3)
            num_times_rec(pool, 1, 3)
            add_b2(4)
            add_b2(5)
            add_b2(6)
            add_b2(7)
        @block.scalar
        def _(act):
            act.preload_act_table_set("natural_log_exp_and_others")
            for k, v in enumerate((w_l1, u_l1)):
                act.dma_start(vec_rows[NC * (k + 2):NC * (k + 3), :], v.rearrange("(c p) -> c p", p=P)).then_inc(vec_loaded, 16)
            act.dma_start(cond_all[:, :, :].rearrange("p b d -> p (b d)"),
                          cond.rearrange("b d -> (b d)").rearrange("(a n) -> a n", a=1).broadcast_to([P, NB * TD])).then_inc(cond_loaded, 16)
            act.dma_start(vec_rows[4 * NC:NV, :], b1.rearrange("(c p) -> c p", p=P)).then_inc(vec_loaded, 16)
            act.dma_start(Wg_nat[:, :], Wg).then_inc(Wg_loaded, 16)

            act.wait_ge(small_dve, 1)
            act.activation(tf[:, 1], tf[:, 0], ACT.Exp, scale=-1.0).then_inc(small_act, 1)
            act.wait_ge(vecs_ready, 1)
            wcols = vecs[:, 0:4 * NC].rearrange("p (l k c) -> p l k c", l=LAYERS, k=2)[:, :, 0, :]
            act.activation(edecay[:, :, :], wcols, ACT.Exp).then_inc(small_act, 1)
            act.wait_ge(small_act, 2)
            act.activation(edecay[:, :, :], edecay[:, :, :], ACT.Exp, scale=-1.0).then_inc(small_act, 1)

            def exps_F(b):
                act.wait_ge(FT_psum, b + 1)
                act.activation(kv[:, b, :, 1, :], chunked(F_bank[b]), ACT.Exp).then_inc(ek_exp, 1)
                act.activation(FT[:, b], chunked(F_bank[b]), ACT.Copy).then_inc(FT_ready, 1)

            def exps_uF(l, b):
                act.wait_ge(FT_ready, b + 1)
                if l:
                    act.wait_ge(num_ready[l - 1], b + 1)
                for c in range(NC):
                    at = NC * (2 * l + 1) + c
                    act.activation(euk[:, b, c], FT[:, b, c], ACT.Exp, bias=vecs[:, at:at + 1]).then_inc(euk_ready[l], 1)

            def scale(l, b, c):
                act.wait_ge(decay_ready, 4)
                act.wait_ge(fwd_done[l], 2 * NC * b + 2 * (c + 1))
                part = scan1[:, b, c, :, 0:T - 1]
                act.activation(part, part, ACT.Copy, scale=one_less_d2[:, l, c, b:b + 1]).then_inc(scaled[l], 1)

            def reciprocal(l, b):
                act.wait_ge(den_ready[l], b + 1)
                rec = scan1[:, b, :, 0, :]
                act.activation(rec, nd[l][:, b, :, 1, :], ACT.Ln).then_inc(ln_done[l], 1)
                act.wait_ge(ln_done[l], b + 1)
                act.activation(rec, rec, ACT.Exp, scale=-1.0).then_inc(rec_ready[l], 1)

            def sigmoids():
                act.preload_act_table_set("sigmoid_and_others")
                for b in range(NB):
                    act.wait_ge(xT_psum, b + 1)
                    act.activation(sig[:, b], chunked(x_bank[b]), ACT.Sigmoid).then_inc(sig_ready, 1)
                act.preload_act_table_set("natural_log_exp_and_others")

            def gate_exp(b):
                act.wait_ge(negmax_ready, b + 1)
                for i in range(NT * b, NT * (b + 1)):
                    act.activation(gexp[:, i], logits[:, i], ACT.Exp, bias=negmax[:, i:i + 1], accum_out=gsum[:, i:i + 1]).then_inc(gsum_ready, 1)

            def evacuate_hmT(i):
                act.wait_ge(hmT_psum, i + 1)
                if i >= 2:
                    act.wait_ge(y_psum, i - 1)
                act.activation(hmT[:, i % 2].rearrange("p m n -> p (m n)"), bank[HMT_BANK + i % 2][:, :], ACT.Copy).then_inc(hmT_ready, 1)

            def evacuate_Wg():
                act.wait_ge(Wg_psum, 1)
                act.activation(WgT[:, :, :].rearrange("p c e -> p (c e)"), bank[MISC_BANK][:, WG_AT:WG_AT + NC * NE], ACT.Copy).then_inc(WgT_ready, 1)

            def evacuate_A(c):
                act.wait_ge(A_psum, c + 1)
                act.activation(AT[:, c], bank[A_bank[c]][:, :], ACT.Copy).then_inc(AT_ready, 1)

            def evacuate_B(k):
                act.wait_ge(B_psum, k + 1)
                act.activation(BT[:, 2 * k:2 * k + 2].rearrange("p m o -> p (m o)"), bank[B_bank[k]][:, :], ACT.Copy,
                               scale=EXTRA_SCALE).then_inc(BT_ready, 1)

            def abs_sum(k):
                act.wait_ge(w_loaded[k], 16)
                if k:
                    act.wait_ge(wsum_ready, k)
                flat = (w1_nat if k == 0 else w2_nat)[:, :, :].rearrange("p a b -> p (a b)")
                act.activation(h32[:, :, :].rearrange("p f t -> p (f t)"), flat, ACT.Abs, accum_out=wsum[:, k:k + 1]).then_inc(wsum_ready, 1)

            def evacuate_wT(k):
                which, n = divmod(k, 2)
                act.wait_ge(qT_psum, k + 1)
                dst = w1T[:, n] if which == 0 else w2T[:, 4 * n:4 * n + 4].rearrange("p f d -> p (f d)")
                act.activation(dst, bank[WT_BANK][:, :].bitcast(BF16), ACT.Copy).then_inc(wT_ready, 1)

            def tanh(b):
                act.wait_ge(x1T_psum, b + 1)
                act.wait_ge(cond_ready, b + 1)
                act.activation(sig[:, b], chunked(x1T_bank[b % 2]), ACT.Tanh, scale=0.5).then_inc(tanh_ready, 1)

            def xin_high(b):
                act.wait_ge(xin_ready, b + 1)
                if b >= 2:
                    act.wait_ge(g_psum, NJ * (b - 1))
                act.activation(xin_hi[:, b % 2], sig[:, b], ACT.Copy, scale=out_scale[:, 1, b:b + 1]).then_inc(xhi_ready, 1)

            def gelus(b, j):
                act.wait_ge(g_psum, NJ * b + j + 1)
                if b:
                    act.wait_ge(hlo_ready, NJ * (b - 1) + j + 1)
                for f in (2 * j, 2 * j + 1):
                    act.activation(h32[:, f], bank[j][:, (f % 2) * T:(f % 2 + 1) * T], ACT.Gelu,
                                   bias=vecs[:, 4 * NC + f:4 * NC + f + 1]).then_inc(h32_ready, 1)

            def h_high(b, j):
                act.wait_ge(h32_ready, NF * b + 2 * j + 2)
                if b >= 2:
                    act.wait_ge(o_psum, NT * (b - 1))
                act.activation(h_hi[:, b % 2, 2 * j:2 * j + 2], h32[:, 2 * j:2 * j + 2], ACT.Copy).then_inc(hhi_ready, 1)

            exps_F(0)
            exps_uF(0, 0)
            evacuate_Wg()
            exps_F(1)
            exps_uF(0, 1)
            scale(0, 0, 0)
            exps_F(2)
            scale(0, 0, 1)
            exps_F(3)
            scale(0, 1, 0)
            sigmoids()
            scale(0, 1, 1)
            reciprocal(0, 0)
            scale(0, 2, 0)
            exps_uF(0, 2)
            reciprocal(0, 1)
            scale(0, 2, 1)
            evacuate_A(0)
            abs_sum(0)
            evacuate_A(1)
            abs_sum(1)
            scale(0, 3, 0)
            exps_uF(0, 3)
            scale(0, 3, 1)
            reciprocal(0, 2)
            evacuate_B(0)
            gate_exp(0)
            evacuate_B(1)
            gate_exp(1)
            scale(1, 0, 0)
            exps_uF(1, 0)
            scale(1, 0, 1)
            exps_uF(1, 1)
            evacuate_wT(0)
            exps_uF(1, 2)
            reciprocal(0, 3)
            evacuate_hmT(0)
            scale(1, 1, 0)
            evacuate_hmT(1)
            evacuate_wT(1)
            exps_uF(1, 3)
            scale(1, 1, 1)
            scale(1, 2, 0)
            gate_exp(2)
            evacuate_hmT(2)
            scale(1, 2, 1)
            evacuate_hmT(3)
            reciprocal(1, 0)
            evacuate_hmT(4)
            scale(1, 3, 0)
            scale(1, 3, 1)
            evacuate_hmT(5)
            gate_exp(3)
            evacuate_wT(2)
            reciprocal(1, 1)
            evacuate_wT(3)
            reciprocal(1, 2)
            evacuate_hmT(6)
            reciprocal(1, 3)
            act.preload_act_table_set("gelu_and_others")
            tanh(0)
            evacuate_hmT(7)
            tanh(1)
            xin_high(0)
            tanh(2)
            xin_high(1)
            gelus(0, 0)
            tanh(3)
            h_high(0, 0)
            gelus(0, 1)
            h_high(0, 1)
            gelus(0, 2)
            xin_high(2)
            h_high(0, 2)
            gelus(0, 3)
            h_high(0, 3)
            gelus(1, 0)
            h_high(1, 0)
            gelus(1, 1)
            h_high(1, 1)
            gelus(1, 2)
            xin_high(3)
            h_high(1, 2)
            gelus(1, 3)
            gelus(2, 0)
            h_high(1, 3)
            h_high(2, 0)
            gelus(2, 1)
            h_high(2, 1)
            gelus(2, 2)
            h_high(2, 2)
            gelus(2, 3)
            h_high(2, 3)
            gelus(3, 0)
            h_high(3, 0)
            gelus(3, 1)
            h_high(3, 1)
            gelus(3, 2)
            h_high(3, 2)
            gelus(3, 3)
            h_high(3, 3)
        @block.vector
        def _(dve):
            dve.wait_ge(cond_loaded, 16)
            dve.tensor_reduce(tf[:, 0], cond_all[:, :, :], AX_X, ALU.add).then_inc(small_dve, 1)
            dve.wait_ge(consts_ready, 2)
            dve.tensor_copy(identb[:, :], ident[:, :]).then_inc(identb_ready, 1)
            dve.wait_ge(vec_psum, 1)
            dve.tensor_copy(vecs[:, :], bank[MISC_BANK][:, VEC_AT:VEC_AT + NV]).then_inc(vecs_ready, 1)
            dve.wait_ge(small_act, 1)
            dve.tensor_scalar(tf[:, 1], tf[:, 1], 1.0, None, ALU.add).then_inc(small_dve, 1)
            dve.wait_ge(small_dve, 2)
            dve.reciprocal(tf[:, 2], tf[:, 1]).then_inc(small_dve, 1)
            dve.wait_ge(small_dve, 3)
            dve.tensor_scalar(out_scale[:, 0], tf[:, 2], -0.2, -0.8, ALU.mult, ALU.add).then_inc(small_dve, 1)
            dve.tensor_scalar(out_scale[:, 1], tf[:, 2], -0.1, -0.4, ALU.mult, ALU.add).then_inc(small_dve, 1)
            dve.tensor_scalar(tf[:, 0], tf[:, 2], 0.5, 0.5, ALU.mult, ALU.add).then_inc(small_dve, 1)
            dve.wait_ge(small_dve, 6)
            dve.wait_ge(small_act, 3)
            for l in range(LAYERS):
                for c in range(NC):
                    dve.tensor_scalar(decay[:, l, c], tf[:, 0], edecay[:, l, c:c + 1], None, ALU.mult).then_inc(small_dve, 1)
            dve.wait_ge(small_dve, 10)
            flat = "p l c b -> p (l c b)"
            dve.scalar_tensor_tensor(one_less_d2[:, :, :, :].rearrange(flat), decay[:, :, :, :].rearrange(flat), -1.0,
                                     decay[:, :, :, :].rearrange(flat), ALU.mult, ALU.mult).then_inc(decay_ready, 3)
            dve.wait_ge(decay_ready, 3)
            dve.tensor_scalar(one_less_d2[:, :, :, :].rearrange(flat), one_less_d2[:, :, :, :].rearrange(flat), 1.0, None,
                              ALU.add).then_inc(decay_ready, 1)

            def keys_values(b):
                dve.wait_ge(ek_exp, b + 1)
                dve.wait_ge(FT_ready, b + 1)
                dve.scalar_tensor_tensor(kv[:, b, :, 0, :], kv[:, b, :, 1, :], EXP30, FT[:, b], ALU.min,
                                         ALU.mult).then_inc(ekv_ready, 1)
                dve.wait_ge(ekv_ready, b + 1)
                dve.tensor_scalar(kv[:, b, :, 1, :], kv[:, b, :, 1, :], EXP30, None, ALU.min).then_inc(kv_ready, 1)

            def forward(l, b, c):
                dve.wait_ge(kv_ready, b + 1)
                if l:
                    dve.wait_ge(ratio_ready[0], b + 1)
                for q in range(2):
                    dve.tensor_tensor_scan(scan1[:, b, c, q], decay[:, l, c, b:b + 1].broadcast_to([P, T]), kv[:, b, c, q],
                                           0.0, ALU.mult, ALU.add).then_inc(fwd_done[l], 1)

            def backward(l, b, c):
                dve.wait_ge(scaled[l], NC * b + c + 1)
                for q in (1, 0):
                    dve.tensor_tensor_scan(nd[l][:, b, c, q, ::-1], decay[:, l, c, b:b + 1].broadcast_to([P, T]),
                                           scan1[:, b, c, q, ::-1], 0.0, ALU.mult, ALU.add).then_inc(bwd_done[l], 1)

            def add_den(l, b):
                dve.wait_ge(clip_ready[l], b + 1)
                dve.wait_ge(bwd_done[l], 2 * NC * (b + 1))
                den = nd[l][:, b, :, 1, :]
                dve.tensor_tensor(den, euk[:, b], den, ALU.add).then_inc(den_ready[l], 1)

            def ratio(l, b):
                dve.wait_ge(dr_ready[l], b + 1)
                dve.wait_ge(q_ready[l], b + 1)
                num = nd[l][:, b, :, 0, :]
                dve.scalar_tensor_tensor(num, scan1[:, b, :, 1, :], 2.0, num, ALU.subtract, ALU.mult).then_inc(ratio_ready[l], 1)
                if l == 0:
                    dve.wait_ge(ratio_ready[l], b + 1)
                    dve.wait_ge(sig_ready, b + 1)
                    dve.scalar_tensor_tensor(num, num, out_scale[:, 0, b:b + 1], sig[:, b], ALU.mult, ALU.mult).then_inc(cond_ready, 1)

            def gate(b):
                both = slice(NT * b, NT * (b + 1))
                dve.wait_ge(logits_psum, b + 1)
                dve.tensor_copy(logits[:, both].rearrange("p n e -> p (n e)"), bank[MISC_BANK][:, LOGIT_AT:LOGIT_AT + NT * NE]).then_inc(logits_ready, 1)
                dve.wait_ge(logits_ready, b + 1)
                for i in range(NT * b, NT * (b + 1)):
                    dve.max(mx8[:, i], logits[:, i]).then_inc(max_ready, 1)
                dve.wait_ge(max_ready, NT * (b + 1))
                dve.tensor_scalar(negmax[:, both], mx8[:, both, 0], -1.0, None, ALU.mult).then_inc(negmax_ready, 1)
                for i in range(NT * b, NT * (b + 1)):
                    dve.max_index(idx8[:, i], mx8[:, i], logits[:, i]).then_inc(idx_ready, 1)
                dve.wait_ge(idx_ready, NT * (b + 1))
                dve.wait_ge(consts_ready, 3 + NE)
                for i in range(NT * b, NT * (b + 1)):
                    dve.tensor_scalar(mask[:, i], iota8[:, :], idx8[:, i, 0:1], None, ALU.is_equal).then_inc(mask_ready, 1)

            def select_expert(i):
                dve.wait_ge(gsum_ready, i + 1)
                dve.reciprocal(grec[:, i:i + 1], gsum[:, i:i + 1]).then_inc(grec_ready, 1)
                dve.wait_ge(grec_ready, i + 1)
                dve.wait_ge(mask_ready, i + 1)
                dve.wait_ge(h_psum, i + 1)
                if i >= 2:
                    dve.wait_ge(hmT_psum, i - 1)
                dve.scalar_tensor_tensor(hm[:, i % 2].rearrange("p (e r) -> p e r", e=NE),
                                         bank[H_BANK + i % 2][:, :].rearrange("p (e r) -> p e r", e=NE), grec[:, i:i + 1],
                                         mask[:, i].rearrange("p (e a) -> p e a", a=1).broadcast_to([P, NE, R]),
                                         ALU.mult, ALU.mult).then_inc(hm_ready, 1)

            def residual(i):
                dve.wait_ge(y_psum, i + 1)
                dve.wait_ge(x_loaded[i // NT], 16)
                dve.tensor_tensor(x_nat[:, i], x_nat[:, i], bank[Y_BANK + i % 2][:, 0:C], ALU.add).then_inc(x1_ready, 1)

            def thresholds():
                dve.wait_ge(wtot_psum, 1)
                dve.tensor_scalar(thr[:, 0], bank[WT_BANK][:, 0:2], 1.0 / (DFF * C), 0.7, ALU.mult, ALU.mult).then_inc(thr_ready, 1)
                dve.wait_ge(thr_ready, 1)
                dve.tensor_scalar(thr[:, 1], thr[:, 0], -1.0, None, ALU.mult).then_inc(thr_ready, 1)

            def negatives(k):
                dve.wait_ge(thr_ready, 2)
                if k:
                    dve.wait_ge(quant_ready, k)
                flat_w = (w1_nat if k == 0 else w2_nat)[:, :, :].rearrange("p a b -> p (a b)")
                dve.tensor_scalar(neg_part[:, :], flat_w, thr[:, 1, k:k + 1], None, ALU.is_le).then_inc(neg_ready, 1)

            def quantise(k):
                dve.wait_ge(neg_ready, k + 1)
                flat_w = (w1_nat if k == 0 else w2_nat)[:, :, :].rearrange("p a b -> p (a b)")
                flat_q = (q1 if k == 0 else q2)[:, :, :].rearrange("p a b -> p (a b)")
                dve.scalar_tensor_tensor(flat_q, flat_w, thr[:, 0, k:k + 1], neg_part[:, :], ALU.is_ge, ALU.subtract).then_inc(quant_ready, 1)

            def ffn_input(b):
                dve.wait_ge(tanh_ready, b + 1)
                dve.wait_ge(ratio_ready[1], b + 1)
                dve.scalar_tensor_tensor(sig[:, b], sig[:, b], 1.0, nd[1][:, b, :, 0, :], ALU.add, ALU.mult).then_inc(xin_ready, 1)

            def xin_low(b):
                dve.wait_ge(xhi_ready, b + 1)
                if b >= 2:
                    dve.wait_ge(g_psum, NJ * (b - 1))
                dve.scalar_tensor_tensor(xin_lo[:, b % 2], sig[:, b], out_scale[:, 1, b:b + 1], xin_hi[:, b % 2].bitcast(F32),
                                         ALU.mult, ALU.subtract).then_inc(xlo_ready, 1)

            def h_low(b, j):
                dve.wait_ge(hhi_ready, NJ * b + j + 1)
                if b >= 2:
                    dve.wait_ge(o_psum, NT * (b - 1))
                dve.tensor_tensor(h_lo[:, b % 2, 2 * j:2 * j + 2], h32[:, 2 * j:2 * j + 2], h_hi[:, b % 2, 2 * j:2 * j + 2].bitcast(F32),
                                  ALU.subtract).then_inc(hlo_ready, 1)

            def result(i):
                dve.wait_ge(o_psum, i + 1)
                dve.wait_ge(x1b_ready, i + 1)
                if i >= 2:
                    dve.wait_ge(out_stored[i % 2], 16 * (i // 2))
                dve.tensor_tensor(outb[:, i % 2], bank[Y_BANK + i % 2][:, 0:C], x1b[:, i], ALU.add).then_inc(out_ready, 1)

            keys_values(0)
            clip_euk(dve, 0, 0)
            forward(0, 0, 0)
            forward(0, 0, 1)
            backward(0, 0, 0)
            forward(0, 1, 0)
            forward(0, 1, 1)
            backward(0, 0, 1)
            add_den(0, 0)
            forward(0, 2, 0)
            times_v(dve, 0, 0)
            forward(0, 2, 1)
            add_num(dve, 0, 0)
            backward(0, 1, 0)
            forward(0, 3, 0)
            forward(0, 3, 1)
            backward(0, 1, 1)
            add_den(0, 1)
            num_times_rec(dve, 0, 0)
            den_times_rec(dve, 0, 0)
            backward(0, 2, 0)
            ratio(0, 0)
            backward(0, 2, 1)
            forward(1, 0, 0)
            gate(0)
            add_den(0, 2)
            ratio(0, 1)
            forward(1, 0, 1)
            thresholds()
            forward(1, 1, 0)
            gate(1)
            negatives(0)
            backward(0, 3, 0)
            quantise(0)
            backward(0, 3, 1)
            select_expert(0)
            add_den(0, 3)
            backward(1, 0, 0)
            select_expert(1)
            ratio(0, 2)
            select_expert(2)
            forward(1, 1, 1)
            residual(0)
            forward(1, 2, 0)
            gate(2)
            forward(1, 2, 1)
            negatives(1)
            residual(1)
            quantise(1)
            select_expert(3)
            backward(1, 0, 1)
            select_expert(4)
            add_den(1, 0)
            backward(1, 1, 0)
            ratio(0, 3)
            residual(2)
            forward(1, 3, 0)
            select_expert(5)
            forward(1, 3, 1)
            gate(3)
            backward(1, 1, 1)
            residual(3)
            backward(1, 2, 0)
            add_den(1, 1)
            backward(1, 2, 1)
            select_expert(6)
            backward(1, 3, 0)
            add_den(1, 2)
            backward(1, 3, 1)
            residual(4)
            add_den(1, 3)
            ratio(1, 0)
            residual(5)
            ratio(1, 1)
            select_expert(7)
            residual(6)
            ffn_input(0)
            ffn_input(1)
            xin_low(0)
            residual(7)
            xin_low(1)
            ratio(1, 2)
            ffn_input(2)
            h_low(0, 0)
            h_low(0, 1)
            xin_low(2)
            h_low(0, 2)
            ratio(1, 3)
            h_low(0, 3)
            ffn_input(3)
            h_low(1, 0)
            h_low(1, 1)
            result(0)
            xin_low(3)
            h_low(1, 2)
            h_low(1, 3)
            result(1)
            h_low(2, 0)
            h_low(2, 1)
            result(2)
            h_low(2, 2)
            result(3)
            h_low(2, 3)
            h_low(3, 0)
            h_low(3, 1)
            result(4)
            h_low(3, 2)
            h_low(3, 3)
            result(5)
            result(6)
            result(7)
        @block.tensor
        def _(pe):
            pe.wait_ge(consts_ready, 2)
            pe.wait_ge(vec_loaded, 16 * 5)
            pe.transpose(bank[MISC_BANK][:, VEC_AT:VEC_AT + NV], vec_rows[:, :], ident[0:NV, 0:NV]).then_inc(vec_psum, 1)

            def transpose_F(b):
                pe.wait_ge(F_loaded[b], 16)
                if b == 3:
                    pe.wait_ge(FT_ready, 1)
                for c in range(NC):
                    for n in range(NT):
                        mm = pe.transpose(bank[F_bank[b]][:, c * T + n * P:c * T + (n + 1) * P],
                                          F_nat[:, b, n, c * P:(c + 1) * P], ident[:, :])
                mm.then_inc(FT_psum, 1)

            def transpose_x(b):
                pe.wait_ge(x_loaded[b], 16)
                for c in range(NC):
                    for n in range(NT):
                        mm = pe.transpose(bank[x_bank[b]][:, c * T + n * P:c * T + (n + 1) * P],
                                          x_nat[:, NT * b + n, c * P:(c + 1) * P], ident[:, :])
                mm.then_inc(xT_psum, 1)

            def transpose_Wg():
                pe.wait_ge(Wg_loaded, 16)
                pe.wait_ge(vecs_ready, 1)
                for c in range(NC):
                    mm = pe.transpose(bank[MISC_BANK][:, WG_AT + NE * c:WG_AT + NE * (c + 1)], Wg_nat[:, c * P:(c + 1) * P], ident[0:NE, 0:NE])
                mm.then_inc(Wg_psum, 1)

            def transpose_A(c):
                pe.wait_ge(A_loaded, 16)
                if c == 0:
                    pe.wait_ge(FT_ready, 2)
                else:
                    pe.wait_ge(sig_ready, 1)
                for m in range(NM):
                    mm = pe.transpose(bank[A_bank[c]][:, m * P:(m + 1) * P], A_nat[:, m, c * P:(c + 1) * P], ident[:, :])
                mm.then_inc(A_psum, 1)

            def transpose_B(k):
                pe.wait_ge(B_loaded, 16 * NC)
                pe.wait_ge(sig_ready, k + 2)
                for m in (2 * k, 2 * k + 1):
                    for o in range(NC):
                        at = (m % 2) * C + o * P
                        mm = pe.transpose(bank[B_bank[k]][:, at:at + P], B_nat[:, o].rearrange("p e r -> p (e r)")[:, m * P:(m + 1) * P], ident[:, :])
                mm.then_inc(B_psum, 1)

            def gate_logits(b):
                pe.wait_ge(cond_ready, b + 1)
                if b == 0:
                    pe.wait_ge(WgT_ready, 1)
                else:
                    pe.wait_ge(logits_ready, b)
                for n in range(NT):
                    at = LOGIT_AT + NE * n
                    for c in range(NC):
                        mm = pe.matmul(bank[MISC_BANK][:, at:at + NE], nd[0][:, b, c, 0, n * P:(n + 1) * P], WgT[:, c],
                                       start=(c == 0), stop=(c == NC - 1))
                mm.then_inc(logits_psum, 1)

            def expert_in(i):
                b, n = divmod(i, NT)
                pe.wait_ge(cond_ready, b + 1)
                if i == 0:
                    pe.wait_ge(AT_ready, NC)
                    pe.wait_ge(BT_ready, 1)
                if i >= 2:
                    pe.wait_ge(hm_ready, i - 1)
                for c in range(NC):
                    mm = pe.matmul(bank[H_BANK + i % 2][:, :], nd[0][:, b, c, 0, n * P:(n + 1) * P], AT[:, c],
                                   start=(c == 0), stop=(c == NC - 1))
                mm.then_inc(h_psum, 1)

            def transpose_hm(i):
                pe.wait_ge(hm_ready, i + 1)
                if i == 0:
                    pe.wait_ge(FT_ready, NB)
                if i >= 2:
                    pe.wait_ge(hmT_ready, i - 1)
                for m in range(NM):
                    mm = pe.transpose(bank[HMT_BANK + i % 2][:, m * P:(m + 1) * P], hm[:, i % 2, m * P:(m + 1) * P], ident[:, :])
                mm.then_inc(hmT_psum, 1)

            def expert_out(i):
                pe.wait_ge(hmT_ready, i + 1)
                if i == 0:
                    pe.wait_ge(BT_ready, 2)
                if i == 1:
                    pe.wait_ge(sig_ready, NB)
                if i >= 2:
                    pe.wait_ge(x1_ready, i - 1)
                for m in range(NM):
                    mm = pe.matmul(bank[Y_BANK + i % 2][:, 0:C], hmT[:, i % 2, m], BT[:, m],
                                   start=(m == 0), stop=(m == NM - 1))
                mm.then_inc(y_psum, 1)

            def weight_totals():
                pe.wait_ge(wsum_ready, 2)
                pe.wait_ge(consts_ready, 3)
                pe.wait_ge(FT_ready, 3)
                pe.matmul(bank[WT_BANK][:, 0:2], ones[:, :], wsum[:, :], start=True, stop=True).then_inc(wtot_psum, 1)

            def transpose_weights(k):
                which, n = divmod(k, 2)
                pe.wait_ge(quant_ready, which + 1)
                pe.wait_ge(identb_ready, 1)
                if k:
                    pe.wait_ge(wT_ready, k)
                for s in range(8):
                    if which == 0:
                        src = q1[:, s, n * P:(n + 1) * P]
                    else:
                        f = 4 * n + s // 2
                        src = q2[:, s % 2, f * P:(f + 1) * P]
                    mm = pe.transpose(bank[WT_BANK][:, :].bitcast(BF16)[:, s * P:(s + 1) * P], src, identb[:, :])
                mm.then_inc(qT_psum, 1)

            def transpose_x1(b):
                pe.wait_ge(x1_ready, NT * (b + 1))
                if b < 2:
                    pe.wait_ge(wT_ready, 4)
                    pe.wait_ge(logits_ready, NB)
                else:
                    pe.wait_ge(tanh_ready, b - 1)
                for c in range(NC):
                    for n in range(NT):
                        mm = pe.transpose(bank[x1T_bank[b % 2]][:, c * T + n * P:c * T + (n + 1) * P],
                                          x_nat[:, NT * b + n, c * P:(c + 1) * P], ident[:, :])
                mm.then_inc(x1T_psum, 1)

            def hidden(b, j):
                pe.wait_ge(xlo_ready, b + 1)
                if b:
                    pe.wait_ge(h32_ready, NF * (b - 1) + 2 * j + 2)
                for f in (2 * j, 2 * j + 1):
                    for c in range(NC):
                        for part in (xin_hi, xin_lo):
                            mm = pe.matmul(bank[j][:, (f % 2) * T:(f % 2 + 1) * T], w1T[:, c, f * P:(f + 1) * P],
                                           part[:, b % 2, c], start=(c == 0 and part is xin_hi),
                                           stop=(c == NC - 1 and part is xin_lo))
                mm.then_inc(g_psum, 1)

            def ffn_out(i):
                b, n = divmod(i, NT)
                if i >= 2:
                    pe.wait_ge(out_ready, i - 1)
                for f in range(NF):
                    pe.wait_ge(hlo_ready, NJ * b + f // 2 + 1)
                    for part in (h_hi, h_lo):
                        mm = pe.matmul(bank[Y_BANK + n][:, 0:C], part[:, b % 2, f, n * P:(n + 1) * P], w2T[:, f],
                                       start=(f == 0 and part is h_hi), stop=(f == NF - 1 and part is h_lo))
                mm.then_inc(o_psum, 1)

            transpose_F(0)
            transpose_x(0)
            transpose_Wg()
            transpose_F(1)
            transpose_x(1)
            transpose_F(2)
            transpose_x(2)
            transpose_F(3)
            transpose_x(3)
            transpose_A(0)
            transpose_B(0)
            transpose_A(1)
            transpose_B(1)
            gate_logits(0)
            weight_totals()
            gate_logits(1)
            expert_in(0)
            expert_in(1)
            transpose_weights(0)
            transpose_hm(0)
            expert_in(2)
            transpose_weights(1)
            transpose_hm(1)
            expert_out(0)
            gate_logits(2)
            expert_out(1)
            transpose_hm(2)
            expert_in(3)
            expert_out(2)
            expert_in(4)
            transpose_hm(3)
            expert_in(5)
            expert_out(3)
            transpose_hm(4)
            gate_logits(3)
            expert_out(4)
            transpose_hm(5)
            expert_in(6)
            transpose_weights(2)
            expert_out(5)
            transpose_weights(3)
            expert_in(7)
            transpose_hm(6)
            transpose_x1(0)
            transpose_x1(1)
            expert_out(6)
            transpose_hm(7)
            transpose_x1(2)
            expert_out(7)
            hidden(0, 0)
            transpose_x1(3)
            hidden(0, 1)
            hidden(0, 2)
            hidden(0, 3)
            hidden(1, 0)
            hidden(1, 1)
            hidden(1, 2)
            hidden(1, 3)
            ffn_out(0)
            hidden(2, 0)
            ffn_out(1)
            hidden(2, 1)
            ffn_out(2)
            hidden(2, 2)
            ffn_out(3)
            hidden(2, 3)
            hidden(3, 0)
            hidden(3, 1)
            hidden(3, 2)
            ffn_out(4)
            hidden(3, 3)
            ffn_out(5)
            ffn_out(6)
            ffn_out(7)


_INS = ['x', 'fside_BxSxS_0', 'cond_512', 'L0_cond_w', 'L0_cond_u', 'L0_ffn_A', 'L0_ffn_Bw', 'L0_ffn_Wg',
        'L1_cond_w', 'L1_cond_u', 'L1_ffn_w1', 'L1_ffn_b1', 'L1_ffn_w2', 'L1_ffn_b2']
_OUTS = [((4, 256, 256), 'float32')]


def kernel(**inputs):
    import numpy as _np
    import concourse.bacc as _bacc
    from concourse import mybir as _mybir
    from concourse.bass_utils import run_bass_kernel_spmd as _run

    nc = _bacc.Bacc("TRN2", target_bir_lowering=False, num_devices=1)
    arrays, args = {}, []
    for name in _INS:
        a = _np.ascontiguousarray(inputs[name])
        arrays[f"in_{name}_dram"] = a
        args.append(nc.dram_tensor(f"in_{name}_dram", a.shape, _mybir.dt.from_np(a.dtype), kind="ExternalInput").ap())
    for i, (shape, dtype) in enumerate(_OUTS):
        dt = _mybir.dt.from_np(_np.dtype(dtype))
        args.append(nc.dram_tensor(f"out_{i}_dram", shape, dt, kind="ExternalOutput").ap())
    adaln_ffn_kernel(nc, *args)
    r = _run(nc, [arrays], core_ids=[0])
    return r.results[0]["out_0_dram"]
```

```python
from contextlib import ExitStack

import concourse.bass as bass
from concourse import mybir

ALU = mybir.AluOpType
ACT = mybir.ActivationFunctionType
F32 = mybir.dt.float32
F32R = mybir.dt.float32r
BF16 = mybir.dt.bfloat16
U32 = mybir.dt.uint32
AX_X = mybir.AxisListType.X

P = 128
EXP30 = 1.0686474581524463e13


def adaln_ffn_kernel(nc, x, fside, cond, w_l0, u_l0, A, Bw, Wg, w_l1, u_l1, w1, b1, w2, b2, out):
    NB, T, C = x.shape
    NE, R, _ = A.shape
    DFF = w1.shape[0]
    TD = cond.shape[1]
    NC = C // P
    NT = T // P
    NI = NB * NT
    ER = NE * R
    NM = ER // P
    NF = DFF // P
    NJ = NF // 2
    NV = 4 * NC
    LAYERS = 2
    EXTRA_SCALE = 4.0
    assert NC == 2 and NT == 2 and ER == 512 and NF == 8 and NB == 4

    with ExitStack() as ctx:
        def sb(name, shape, dt=F32, where=ctx):
            return where.enter_context(nc.sbuf_tensor(name, shape, dt))

        def sem(name):
            return ctx.enter_context(nc.semaphore(name))

        bank = [ctx.enter_context(nc.psum_tensor(f"bank{k}", [P, 512], F32)) for k in range(8)]

        ident = sb("ident", [P, P])
        identb = sb("identb", [P, P], BF16)
        expert_of = sb("expert_of", [P, P])
        vecs = sb("vecs", [P, NV])
        b1T = sb("b1T", [P, NF])
        tf = sb("tf", [P, 3, NB])
        out_scale = sb("out_scale", [P, NB])
        edecay = sb("edecay", [P, LAYERS, NC])
        decay = sb("decay", [P, LAYERS, NC, NB])
        one_less_d2 = sb("one_less_d2", [P, LAYERS, NC, NB])
        b2_all = sb("b2_all", [P, C])
        x_nat = sb("x_nat", [P, NI, C])
        FT = sb("FT", [P, NB, NC, T])
        vs = sb("vs", [P, NB, NC, T])
        kv = sb("kv", [P, NB, NC, 2, T])
        euk = sb("euk", [P, NB, NC, T])
        scan1 = sb("scan1", [P, NB, NC, 2, T])
        nd = [sb(f"nd{l}", [P, NB, NC, 2, T]) for l in range(LAYERS)]
        sig = sb("sig", [P, NB, NC, T])
        xin_hi = sb("xin_hi", [P, 2, NC, T], F32R)
        xin_lo = sb("xin_lo", [P, 2, NC, T], F32R)
        WgT = sb("WgT", [P, NC, NE])
        AT = sb("AT", [P, NC, ER])
        BT = sb("BT", [P, NM, C])
        w1T = sb("w1T", [P, NC, DFF], F32R)
        w2T = sb("w2T", [P, NF, C], F32R)
        pos1 = sb("pos1", [P, NF, C], BF16)
        pos2 = sb("pos2", [P, NC, DFF], BF16)
        wsum = sb("wsum", [P, 2])
        thr = sb("thr", [P, 2, 2])
        mx8 = sb("mx8", [P, NI, NE])
        idx8 = sb("idx8", [P, NI, NE], U32)
        negmax = sb("negmax", [P, NI])
        logits = sb("logits", [P, NI, NE])
        gexp = sb("gexp", [P, NI, NE])
        gsum = sb("gsum", [P, NI])
        grec = sb("grec", [P, NI])
        mask = sb("mask", [P, 2 * NT, P], BF16)
        mask_rows = sb("mask_rows", [P, 2, T], BF16)
        hm = sb("hm", [P, 2, NM, T])
        h32 = sb("h32", [P, NF, T])
        outb = sb("outb", [P, 2, C])
        early = ExitStack()
        minus_identb = sb("minus_identb", [P, P], BF16, early)
        cond_all = sb("cond_all", [P, NB, TD], F32, early)
        b1_rows = sb("b1_rows", [NF, P], F32, early)
        vec_rows = sb("vec_rows", [NV, P], F32, early)
        ones = sb("ones", [P, P], F32, early)
        w1_nat = sb("w1_nat", [P, NF, C], F32, early)
        w2_nat = sb("w2_nat", [P, NC, DFF], F32, early)
        neg_part = sb("neg_part", [P, 2 * DFF], BF16, early)
        A_nat = sb("A_nat", [P, NM, C], F32, early)
        B_nat = sb("B_nat", [P, NC, NE, R], F32, early)
        Wg_nat = sb("Wg_nat", [NE, C], F32, early)
        F_nat = sb("F_nat", [P, NB, NT, C], F32, early)
        early.close()
        h_hi = sb("h_hi", [P, 2, NF, T], F32R)
        h_lo = sb("h_lo", [P, 2, NF, T], F32R)
        x1b = sb("x1b", [P, NI, C])

        def per(kind, n):
            return [sem(f"{kind}_{k}") for k in range(n)]

        F_loaded, x_loaded = per("F_loaded", NB), per("x_loaded", NB)
        b1_loaded, b1T_ready = sem("b1_loaded"), sem("b1T_ready")
        vec_loaded, cond_loaded, b2_loaded = sem("vec_loaded"), sem("cond_loaded"), sem("b2_loaded")
        Wg_loaded, A_loaded, B_loaded = sem("Wg_loaded"), sem("A_loaded"), sem("B_loaded")
        w_loaded = per("w_loaded", 2)
        consts_ready, identb_ready = sem("consts_ready"), sem("identb_ready")
        FT_psum, xT_psum = sem("FT_psum"), sem("xT_psum")
        vec_psum, vecs_ready = sem("vec_psum"), sem("vecs_ready")
        small_dve, small_act, decay_ready = sem("small_dve"), sem("small_act"), sem("decay_ready")
        ek_exp, ekv_ready = sem("ek_exp"), sem("ekv_ready")
        ek_ready, vs_ready, qsig_ready = sem("ek_ready"), sem("vs_ready"), sem("qsig_ready")
        FT_ready, sig_ready = sem("FT_ready"), sem("sig_ready")
        euk_ready = per("euk_ready", LAYERS)
        fwd_done, scaled, bwd_done = per("fwd_done", LAYERS), per("scaled", LAYERS), per("bwd_done", LAYERS)
        clip_ready = per("clip_ready", LAYERS)
        den_ready, eukv_ready, num_ready = per("den_ready", LAYERS), per("eukv_ready", LAYERS), per("num_ready", LAYERS)
        ln_done, rec_ready = per("ln_done", LAYERS), per("rec_ready", LAYERS)
        dr_ready, q_ready, ratio_ready = per("dr_ready", LAYERS), per("q_ready", LAYERS), per("ratio_ready", LAYERS)
        Wg_psum, A_psum, B_psum = sem("Wg_psum"), sem("A_psum"), sem("B_psum")
        WgT_ready, AT_ready, BT_ready = sem("WgT_ready"), sem("AT_ready"), sem("BT_ready")
        wsum_ready, wtot_psum, thr_ready = sem("wsum_ready"), sem("wtot_psum"), sem("thr_ready")
        neg_ready, pos_ready = sem("neg_ready"), sem("pos_ready")
        qT_psum, wT_ready = sem("qT_psum"), sem("wT_ready")
        logits_ready = sem("logits_ready")
        logits_psum, h_psum = sem("logits_psum"), sem("h_psum")
        max_ready, negmax_ready, idx_ready = sem("max_ready"), sem("negmax_ready"), sem("idx_ready")
        mask_ready, gsum_ready, grec_ready = sem("mask_ready"), sem("gsum_ready"), sem("grec_ready")
        hm_ready, mask_psum, mask_copied = sem("hm_ready"), sem("mask_psum"), sem("mask_copied")
        y_psum, x1_ready, x1b_ready = sem("y_psum"), sem("x1_ready"), sem("x1b_ready")
        x1T_psum, tanh_ready, xin_ready = sem("x1T_psum"), sem("tanh_ready"), sem("xin_ready")
        xhi_ready, xlo_ready = sem("xhi_ready"), sem("xlo_ready")
        g_psum, h32_ready, hhi_ready, hlo_ready = sem("g_psum"), sem("h32_ready"), sem("hhi_ready"), per("hlo_ready", NJ)
        o_psum, out_ready = sem("o_psum"), sem("out_ready")
        out_stored = per("out_stored", 2)

        F_bank = [0, 1, 7, 0]
        x_bank = [2, 3, 4, 5]
        A_bank, B_bank = [1, 2], [3, 4]
        WT_BANK = 7
        x1T_bank = [6, 7]
        MASK_BANK, H_BANK, Y_BANK, MISC_BANK = 0, 2, 4, 6
        VEC_AT, WG_AT, B1_AT, LOGIT_AT = 0, 32, 64, 128

        def chunked(k):
            return bank[k][:, :].rearrange("p (c t) -> p c t", c=NC)

        def in_turn(eng, done, b):
            if b:
                eng.wait_ge(done, b)

        def scale_wait(eng, l, b, c):
            eng.wait_ge(decay_ready, 4)
            eng.wait_ge(fwd_done[l], 2 * NC * b + 2 * (c + 1))
            in_turn(eng, scaled[l], NC * b + c)

        def scale_by(eng, l, b, c):
            scale_wait(eng, l, b, c)
            part = scan1[:, b, c, :, 0:T - 1]
            eng.tensor_scalar(part, part, one_less_d2[:, l, c, b:b + 1], 1.0, ALU.mult, ALU.mult).then_inc(scaled[l], 1)

        def scale_values(eng, b):
            eng.wait_ge(FT_ready, b + 1)
            eng.wait_ge(small_dve, 4)
            in_turn(eng, vs_ready, b)
            eng.tensor_scalar(vs[:, b], FT[:, b], out_scale[:, b:b + 1], 1.0, ALU.mult, ALU.mult).then_inc(vs_ready, 1)

        def times_values(eng, b):
            eng.wait_ge(vs_ready, b + 1)
            eng.wait_ge(ek_ready, b + 1)
            in_turn(eng, ekv_ready, b)
            eng.tensor_tensor(kv[:, b, :, 0, :], kv[:, b, :, 1, :], vs[:, b], ALU.mult).then_inc(ekv_ready, 1)

        def add_b2(eng, i):
            eng.wait_ge(b2_loaded, 16)
            eng.wait_ge(x1_ready, i + 1)
            in_turn(eng, x1b_ready, i)
            eng.tensor_tensor(x1b[:, i], x_nat[:, i], b2_all[:, :], ALU.add).then_inc(x1b_ready, 1)

        def clip_euk(eng, l, b):
            eng.wait_ge(euk_ready[l], NC * b + NC)
            in_turn(eng, clip_ready[l], b)
            eng.tensor_scalar(euk[:, b], euk[:, b], EXP30, None, ALU.min).then_inc(clip_ready[l], 1)

        def add_den(eng, l, b):
            eng.wait_ge(clip_ready[l], b + 1)
            eng.wait_ge(bwd_done[l], 2 * NC * (b + 1))
            in_turn(eng, den_ready[l], b)
            den = nd[l][:, b, :, 1, :]
            eng.tensor_tensor(den, euk[:, b], den, ALU.add).then_inc(den_ready[l], 1)

        def times_v(eng, l, b):
            eng.wait_ge(den_ready[l], b + 1)
            in_turn(eng, eukv_ready[l], b)
            if eng is nc.vector and b == 0:
                eng.scalar_tensor_tensor(euk[:, b], euk[:, b], out_scale[:, b:b + 1], FT[:, b], ALU.mult, ALU.mult).then_inc(eukv_ready[l], 1)
            else:
                eng.wait_ge(vs_ready, b + 1)
                eng.tensor_tensor(euk[:, b], euk[:, b], vs[:, b], ALU.mult).then_inc(eukv_ready[l], 1)

        def add_num(eng, l, b):
            num = nd[l][:, b, :, 0, :]
            eng.wait_ge(bwd_done[l], 2 * NC * (b + 1))
            eng.wait_ge(eukv_ready[l], b + 1)
            in_turn(eng, num_ready[l], b)
            eng.tensor_tensor(num, num, euk[:, b], ALU.add).then_inc(num_ready[l], 1)

        def den_times_rec(eng, l, b):
            eng.wait_ge(rec_ready[l], b + 1)
            in_turn(eng, dr_ready[l], b)
            eng.tensor_tensor(scan1[:, b, :, 1, :], nd[l][:, b, :, 1, :], scan1[:, b, :, 0, :], ALU.mult).then_inc(dr_ready[l], 1)

        def num_times_rec(eng, l, b):
            num = nd[l][:, b, :, 0, :]
            eng.wait_ge(rec_ready[l], b + 1)
            eng.wait_ge(num_ready[l], b + 1)
            in_turn(eng, q_ready[l], b)
            eng.tensor_tensor(num, num, scan1[:, b, :, 0, :], ALU.mult).then_inc(q_ready[l], 1)

        def times_sigmoid(eng, b):
            num = nd[0][:, b, :, 0, :]
            eng.wait_ge(q_ready[0], b + 1)
            eng.wait_ge(sig_ready, b + 1)
            in_turn(eng, qsig_ready, b)
            eng.tensor_tensor(num, num, sig[:, b], ALU.mult).then_inc(qsig_ready, 1)

        def xin_low(eng, b):
            eng.wait_ge(xhi_ready, b + 1)
            if b >= 2:
                eng.wait_ge(g_psum, NJ * (b - 1))
            in_turn(eng, xlo_ready, b)
            eng.tensor_tensor(xin_lo[:, b % 2], sig[:, b], xin_hi[:, b % 2].bitcast(F32), ALU.subtract).then_inc(xlo_ready, 1)

        def h_low(eng, b, j):
            eng.wait_ge(hhi_ready, NJ * b + j + 1)
            if b >= 2:
                eng.wait_ge(o_psum, NT * (b - 1))
            eng.tensor_tensor(h_lo[:, b % 2, 2 * j:2 * j + 2], h32[:, 2 * j:2 * j + 2], h_hi[:, b % 2, 2 * j:2 * j + 2].bitcast(F32),
                              ALU.subtract).then_inc(hlo_ready[j], 1)

        block = ctx.enter_context(nc.Block())

        @block.sync
        def _(sp):
            F_tiles = fside.rearrange("b (n p) c -> b p n c", p=P)
            x_tiles = x.rearrange("b (n p) c -> b p n c", p=P)
            sp.dma_start(F_nat[:, 0], F_tiles[0]).then_inc(F_loaded[0], 16)
            sp.dma_start(cond_all[:, :, :].rearrange("p b d -> p (b d)"),
                         cond.rearrange("b d -> (b d)").rearrange("(a n) -> a n", a=1).broadcast_to([P, NB * TD])).then_inc(cond_loaded, 16)
            for b in range(NB):
                sp.dma_start(x_nat[:, NT * b:NT * (b + 1)], x_tiles[b]).then_inc(x_loaded[b], 16)
            sp.dma_start(F_nat[:, 1], F_tiles[1]).then_inc(F_loaded[1], 16)
            sp.dma_start(Wg_nat[:, :], Wg).then_inc(Wg_loaded, 16)
            sp.dma_start(b1_rows[:, :], b1.rearrange("(c p) -> c p", p=P)).then_inc(b1_loaded, 16)
            sp.dma_start(A_nat[:, :, :], A.rearrange("e r c -> (e r) c").rearrange("(m p) c -> p m c", p=P)).then_inc(A_loaded, 16)
            for c in range(NC):
                sp.dma_start(B_nat[:, c], Bw[:, c * P:(c + 1) * P, :].rearrange("e o r -> o e r")).then_inc(B_loaded, 16)
            for b in range(2, NB):
                sp.dma_start(F_nat[:, b], F_tiles[b]).then_inc(F_loaded[b], 16)
            sp.dma_start(w1_nat[:, :, :], w1.rearrange("(n p) c -> p n c", p=P)).then_inc(w_loaded[0], 16)
            sp.dma_start(w2_nat[:, :, :], w2.rearrange("(n p) f -> p n f", p=P)).then_inc(w_loaded[1], 16)
            sp.dma_start(b2_all[:, :], b2.rearrange("(a n) -> a n", a=1).broadcast_to([P, C])).then_inc(b2_loaded, 16)
            out_tiles = out.rearrange("b (n p) c -> (b n) p c", p=P)
            for i in range(NI):
                sp.wait_ge(out_ready, i + 1)
                sp.dma_start(out_tiles[i], outb[:, i % 2]).then_inc(out_stored[i % 2], 16)
            for k in range(2):
                sp.wait_ge(out_stored[k], 16 * NI // 2)

        @block.gpsimd
        def _(pool):
            pool.memset(ident[:, :], 0.0).then_inc(consts_ready, 1)
            pool.wait_ge(consts_ready, 1)
            pool.affine_select(out=ident[:, :], in_=ident[:, :], compare_op=ALU.not_equal, fill=1.0, base=0,
                               pattern=[[-1, P]], channel_multiplier=1).then_inc(consts_ready, 1)
            pool.memset(ones[:, :], 1.0).then_inc(consts_ready, 1)
            for e in range(NE):
                pool.memset(expert_of[:, e * P // NE:(e + 1) * P // NE], float(e)).then_inc(consts_ready, 1)

            scale_by(pool, 0, 0, 1)
            times_v(pool, 0, 0)
            scale_values(pool, 1)
            den_times_rec(pool, 0, 0)
            scale_values(pool, 2)
            scale_by(pool, 0, 1, 0)
            times_values(pool, 2)
            scale_by(pool, 0, 1, 1)
            times_sigmoid(pool, 0)
            scale_values(pool, 3)
            times_values(pool, 3)
            times_v(pool, 0, 1)
            den_times_rec(pool, 0, 1)
            add_num(pool, 0, 1)
            num_times_rec(pool, 0, 1)
            times_sigmoid(pool, 1)
            add_den(pool, 0, 2)
            times_v(pool, 0, 2)
            add_num(pool, 0, 2)
            den_times_rec(pool, 0, 2)
            num_times_rec(pool, 0, 2)
            times_sigmoid(pool, 2)
            times_v(pool, 0, 3)
            den_times_rec(pool, 0, 3)
            add_num(pool, 0, 3)
            scale_by(pool, 1, 0, 1)
            num_times_rec(pool, 0, 3)
            add_den(pool, 1, 0)
            times_sigmoid(pool, 3)
            times_v(pool, 1, 0)
            den_times_rec(pool, 1, 0)
            add_num(pool, 1, 0)
            add_den(pool, 1, 1)
            num_times_rec(pool, 1, 0)
            times_v(pool, 1, 1)
            den_times_rec(pool, 1, 1)
            add_num(pool, 1, 1)
            den_times_rec(pool, 1, 2)
            num_times_rec(pool, 1, 1)
            num_times_rec(pool, 1, 2)
            xin_low(pool, 1)
            scale_by(pool, 1, 3, 0)
            h_low(pool, 0, 0)
            add_b2(pool, 3)
            h_low(pool, 0, 1)
            add_b2(pool, 4)
            scale_by(pool, 1, 3, 1)
            h_low(pool, 0, 3)
            times_v(pool, 1, 3)
            add_num(pool, 1, 3)
            add_b2(pool, 7)
            h_low(pool, 1, 3)
            num_times_rec(pool, 1, 3)
        @block.scalar
        def _(act):
            act.preload_act_table_set("natural_log_exp_and_others")

            def load_rows(k, v):
                act.dma_start(vec_rows[NC * k:NC * (k + 1), :], v.rearrange("(c p) -> c p", p=P)).then_inc(vec_loaded, 16)

            load_rows(0, w_l0)
            load_rows(2, w_l1)
            load_rows(1, u_l0)
            load_rows(3, u_l1)

            def cond_exp():
                act.wait_ge(small_dve, 1)
                act.activation(tf[:, 1], tf[:, 0], ACT.Exp, scale=-1.0).then_inc(small_act, 1)

            def decay_exps():
                act.wait_ge(vecs_ready, 1)
                wcols = vecs[:, 0:4 * NC].rearrange("p (l k c) -> p l k c", l=LAYERS, k=2)[:, :, 0, :]
                act.activation(edecay[:, :, :], wcols, ACT.Exp).then_inc(small_act, 1)
                act.wait_ge(small_act, 2)
                act.activation(edecay[:, :, :], edecay[:, :, :], ACT.Exp, scale=-1.0).then_inc(small_act, 1)

            def exps_F(b):
                act.wait_ge(FT_psum, b + 1)
                act.activation(kv[:, b, :, 1, :], chunked(F_bank[b]), ACT.Exp).then_inc(ek_exp, 1)
                act.activation(FT[:, b], chunked(F_bank[b]), ACT.Copy).then_inc(FT_ready, 1)

            def exps_uF(l, b):
                act.wait_ge(vecs_ready, 1)
                act.wait_ge(FT_ready, b + 1)
                if l:
                    act.wait_ge(num_ready[l - 1], b + 1)
                for c in range(NC):
                    at = NC * (2 * l + 1) + c
                    act.activation(euk[:, b, c], FT[:, b, c], ACT.Exp, bias=vecs[:, at:at + 1]).then_inc(euk_ready[l], 1)

            def scale(l, b, c):
                scale_wait(act, l, b, c)
                part = scan1[:, b, c, :, 0:T - 1]
                act.activation(part, part, ACT.Copy, scale=one_less_d2[:, l, c, b:b + 1]).then_inc(scaled[l], 1)

            def reciprocal(l, b):
                act.wait_ge(den_ready[l], b + 1)
                rec = scan1[:, b, :, 0, :]
                act.activation(rec, nd[l][:, b, :, 1, :], ACT.Ln).then_inc(ln_done[l], 1)
                act.wait_ge(ln_done[l], b + 1)
                act.activation(rec, rec, ACT.Exp, scale=-1.0).then_inc(rec_ready[l], 1)

            def sigmoids():
                act.preload_act_table_set("sigmoid_and_others")
                for b in range(NB):
                    act.wait_ge(xT_psum, b + 1)
                    act.activation(sig[:, b], chunked(x_bank[b]), ACT.Sigmoid).then_inc(sig_ready, 1)
                act.preload_act_table_set("natural_log_exp_and_others")

            def gate_exp(b):
                act.wait_ge(negmax_ready, b + 1)
                for i in range(NT * b, NT * (b + 1)):
                    act.activation(gexp[:, i], logits[:, i], ACT.Exp, bias=negmax[:, i:i + 1], accum_out=gsum[:, i:i + 1]).then_inc(gsum_ready, 1)

            def copy_mask(b):
                act.wait_ge(mask_psum, b + 1)
                if b >= 2:
                    act.wait_ge(hm_ready, 2 * (b - 1))
                act.activation(mask_rows[:, b % 2], bank[MASK_BANK + b % 2][:, 0:P].bitcast(BF16), ACT.Copy).then_inc(mask_copied, 1)

            def evacuate_Wg():
                act.wait_ge(Wg_psum, 1)
                act.activation(b1T[:, :], bank[MISC_BANK][:, B1_AT:B1_AT + NF], ACT.Copy).then_inc(b1T_ready, 1)
                act.activation(WgT[:, :, :].rearrange("p c e -> p (c e)"), bank[MISC_BANK][:, WG_AT:WG_AT + NC * NE], ACT.Copy).then_inc(WgT_ready, 1)

            def evacuate_A(c):
                act.wait_ge(A_psum, c + 1)
                act.activation(AT[:, c], bank[A_bank[c]][:, :], ACT.Copy).then_inc(AT_ready, 1)

            def evacuate_B(k):
                act.wait_ge(B_psum, k + 1)
                act.activation(BT[:, 2 * k:2 * k + 2].rearrange("p m o -> p (m o)"), bank[B_bank[k]][:, :], ACT.Copy,
                               scale=EXTRA_SCALE).then_inc(BT_ready, 1)

            def abs_sum(k):
                act.wait_ge(w_loaded[k], 16)
                if k:
                    act.wait_ge(wsum_ready, k)
                flat = (w1_nat if k == 0 else w2_nat)[:, :, :].rearrange("p a b -> p (a b)")
                act.activation(h32[:, :, :].rearrange("p f t -> p (f t)"), flat, ACT.Abs, accum_out=wsum[:, k:k + 1]).then_inc(wsum_ready, 1)

            def evacuate_wT(k):
                act.wait_ge(qT_psum, k + 1)
                if k < 4:
                    dst = w1T[:, k // 2, 4 * P * (k % 2):4 * P * (k % 2 + 1)]
                else:
                    dst = w2T[:, 2 * (k - 4):2 * (k - 4) + 2].rearrange("p f d -> p (f d)")
                act.activation(dst, bank[WT_BANK][:, :], ACT.Copy, scale=0.5 if k < 4 else 1.0).then_inc(wT_ready, 1)

            def tanh(b):
                act.wait_ge(x1T_psum, b + 1)
                act.wait_ge(ratio_ready[0], b + 1)
                act.activation(sig[:, b], chunked(x1T_bank[b % 2]), ACT.Tanh, scale=0.5).then_inc(tanh_ready, 1)

            def xin_high(b):
                act.wait_ge(xin_ready, b + 1)
                if b >= 2:
                    act.wait_ge(g_psum, NJ * (b - 1))
                act.activation(xin_hi[:, b % 2], sig[:, b], ACT.Copy).then_inc(xhi_ready, 1)

            def gelus(b, j):
                act.wait_ge(b1T_ready, 1)
                act.wait_ge(g_psum, NJ * b + j + 1)
                if b:
                    act.wait_ge(hlo_ready[j], b)
                for f in (2 * j, 2 * j + 1):
                    act.activation(h32[:, f], bank[j][:, (f % 2) * T:(f % 2 + 1) * T], ACT.Gelu,
                                   bias=b1T[:, f:f + 1]).then_inc(h32_ready, 1)

            def h_high(b, j):
                act.wait_ge(h32_ready, NF * b + 2 * j + 2)
                if b == 0:
                    act.wait_ge(qT_psum, 8)
                elif b >= 2:
                    act.wait_ge(o_psum, NT * (b - 1))
                act.activation(h_hi[:, b % 2, 2 * j:2 * j + 2], h32[:, 2 * j:2 * j + 2], ACT.Copy).then_inc(hhi_ready, 1)

            exps_F(0)
            cond_exp()
            exps_uF(0, 0)
            decay_exps()
            sigmoids()
            exps_F(1)
            reciprocal(0, 0)
            exps_F(2)
            exps_uF(0, 1)
            exps_F(3)
            abs_sum(0)
            evacuate_Wg()
            abs_sum(1)
            scale(0, 2, 0)
            reciprocal(0, 1)
            exps_uF(0, 2)
            evacuate_A(0)
            exps_uF(0, 3)
            evacuate_A(1)
            evacuate_B(0)
            scale(0, 2, 1)
            evacuate_B(1)
            scale(0, 3, 0)
            exps_uF(1, 0)
            scale(0, 3, 1)
            exps_uF(1, 1)
            copy_mask(0)
            reciprocal(0, 2)
            gate_exp(0)
            evacuate_wT(0)
            exps_uF(1, 2)
            gate_exp(1)
            copy_mask(1)
            evacuate_wT(1)
            evacuate_wT(2)
            reciprocal(0, 3)
            evacuate_wT(3)
            scale(1, 0, 0)
            gate_exp(2)
            copy_mask(2)
            exps_uF(1, 3)
            scale(1, 1, 0)
            scale(1, 1, 1)
            reciprocal(1, 0)
            scale(1, 2, 0)
            evacuate_wT(4)
            scale(1, 2, 1)
            evacuate_wT(5)
            evacuate_wT(6)
            reciprocal(1, 1)
            evacuate_wT(7)
            copy_mask(3)
            gate_exp(3)
            reciprocal(1, 2)
            act.preload_act_table_set("gelu_and_others")
            tanh(0)
            tanh(1)
            xin_high(0)
            xin_high(1)
            gelus(0, 0)
            h_high(0, 0)
            gelus(0, 1)
            gelus(0, 2)
            h_high(0, 1)
            gelus(0, 3)
            tanh(2)
            gelus(1, 0)
            h_high(0, 2)
            xin_high(2)
            h_high(0, 3)
            gelus(1, 1)
            h_high(1, 0)
            gelus(1, 2)
            h_high(1, 1)
            gelus(1, 3)
            h_high(1, 2)
            act.preload_act_table_set("natural_log_exp_and_others")
            h_high(1, 3)
            reciprocal(1, 3)
            act.preload_act_table_set("gelu_and_others")
            gelus(2, 0)
            tanh(3)
            h_high(2, 0)
            gelus(2, 1)
            xin_high(3)
            gelus(2, 2)
            h_high(2, 1)
            gelus(2, 3)
            h_high(2, 2)
            gelus(3, 0)
            h_high(2, 3)
            gelus(3, 1)
            h_high(3, 0)
            gelus(3, 2)
            h_high(3, 1)
            gelus(3, 3)
            h_high(3, 2)
            h_high(3, 3)
        @block.vector
        def _(dve):
            dve.wait_ge(cond_loaded, 16)
            dve.tensor_reduce(tf[:, 0], cond_all[:, :, :], AX_X, ALU.add).then_inc(small_dve, 1)
            dve.wait_ge(consts_ready, 2)
            dve.tensor_copy(identb[:, :], ident[:, :]).then_inc(identb_ready, 1)
            dve.tensor_scalar(minus_identb[:, :], ident[:, :], -1.0, None, ALU.mult).then_inc(identb_ready, 1)

            def vectors():
                dve.wait_ge(vec_psum, 1)
                dve.tensor_copy(vecs[:, :], bank[MISC_BANK][:, VEC_AT:VEC_AT + NV]).then_inc(vecs_ready, 1)

            def scales():
                dve.wait_ge(small_act, 1)
                dve.tensor_scalar(tf[:, 1], tf[:, 1], 1.0, None, ALU.add).then_inc(small_dve, 1)
                dve.wait_ge(small_dve, 2)
                dve.reciprocal(tf[:, 2], tf[:, 1]).then_inc(small_dve, 1)
                dve.wait_ge(small_dve, 3)
                dve.tensor_scalar(out_scale[:, :], tf[:, 2], -0.2, -0.8, ALU.mult, ALU.add).then_inc(small_dve, 1)
                dve.tensor_scalar(tf[:, 0], tf[:, 2], 0.5, 0.5, ALU.mult, ALU.add).then_inc(small_dve, 1)

            def decays():
                dve.wait_ge(small_dve, 5)
                dve.wait_ge(small_act, 3)
                for l in range(LAYERS):
                    for c in range(NC):
                        dve.tensor_scalar(decay[:, l, c], tf[:, 0], edecay[:, l, c:c + 1], None, ALU.mult).then_inc(small_dve, 1)
                dve.wait_ge(small_dve, 9)
                flat = "p l c b -> p (l c b)"
                dve.scalar_tensor_tensor(one_less_d2[:, :, :, :].rearrange(flat), decay[:, :, :, :].rearrange(flat), -1.0,
                                         decay[:, :, :, :].rearrange(flat), ALU.mult, ALU.mult).then_inc(decay_ready, 3)
                dve.wait_ge(decay_ready, 3)
                dve.tensor_scalar(one_less_d2[:, :, :, :].rearrange(flat), one_less_d2[:, :, :, :].rearrange(flat), 1.0, None,
                                  ALU.add).then_inc(decay_ready, 1)

            def keys_values(b):
                dve.wait_ge(ek_exp, b + 1)
                dve.wait_ge(FT_ready, b + 1)
                dve.tensor_scalar(kv[:, b, :, 1, :], kv[:, b, :, 1, :], EXP30, None, ALU.min).then_inc(ek_ready, 1)
                if b == 0:
                    dve.wait_ge(ek_ready, 1)
                    dve.scalar_tensor_tensor(kv[:, b, :, 0, :], kv[:, b, :, 1, :], out_scale[:, b:b + 1], FT[:, b], ALU.mult,
                                             ALU.mult).then_inc(ekv_ready, 1)

            def forward(l, b, c):
                dve.wait_ge(ekv_ready, b + 1)
                dve.wait_ge(ek_ready, b + 1)
                if l:
                    dve.wait_ge(ratio_ready[0], b + 1)
                for q in range(2):
                    dve.tensor_tensor_scan(scan1[:, b, c, q], decay[:, l, c, b:b + 1].broadcast_to([P, T]), kv[:, b, c, q],
                                           0.0, ALU.mult, ALU.add).then_inc(fwd_done[l], 1)

            def backward(l, b, c):
                dve.wait_ge(scaled[l], NC * b + c + 1)
                for q in (1, 0):
                    dve.tensor_tensor_scan(nd[l][:, b, c, q, ::-1], decay[:, l, c, b:b + 1].broadcast_to([P, T]),
                                           scan1[:, b, c, q, ::-1], 0.0, ALU.mult, ALU.add).then_inc(bwd_done[l], 1)

            def ratio(l, b):
                dve.wait_ge(dr_ready[l], b + 1)
                if l == 0:
                    dve.wait_ge(qsig_ready, b + 1)
                else:
                    dve.wait_ge(q_ready[l], b + 1)
                num = nd[l][:, b, :, 0, :]
                dve.scalar_tensor_tensor(num, scan1[:, b, :, 1, :], 2.0, num, ALU.subtract, ALU.mult).then_inc(ratio_ready[l], 1)

            def gate(b):
                both = slice(NT * b, NT * (b + 1))
                dve.wait_ge(logits_psum, b + 1)
                dve.tensor_copy(logits[:, both].rearrange("p n e -> p (n e)"), bank[MISC_BANK][:, LOGIT_AT:LOGIT_AT + NT * NE]).then_inc(logits_ready, 1)
                dve.wait_ge(logits_ready, b + 1)
                for i in range(NT * b, NT * (b + 1)):
                    dve.max(mx8[:, i], logits[:, i]).then_inc(max_ready, 1)
                dve.wait_ge(max_ready, NT * (b + 1))
                dve.tensor_scalar(negmax[:, both], mx8[:, both, 0], -1.0, None, ALU.mult).then_inc(negmax_ready, 1)
                for i in range(NT * b, NT * (b + 1)):
                    dve.max_index(idx8[:, i], mx8[:, i], logits[:, i]).then_inc(idx_ready, 1)
                dve.wait_ge(idx_ready, NT * (b + 1))
                dve.wait_ge(consts_ready, 3 + NE)
                if b >= 2:
                    dve.wait_ge(mask_psum, b - 1)
                for i in range(NT * b, NT * (b + 1)):
                    dve.tensor_scalar(mask[:, i % (2 * NT)], expert_of[:, :], idx8[:, i, 0:1], None, ALU.is_equal).then_inc(mask_ready, 1)

            def probability(b):
                both = slice(NT * b, NT * (b + 1))
                dve.wait_ge(gsum_ready, NT * (b + 1))
                dve.reciprocal(grec[:, both], gsum[:, both]).then_inc(grec_ready, 1)

            def select_expert(b, k):
                dve.wait_ge(h_psum, 2 * b + k + 1)
                dve.wait_ge(mask_copied, b + 1)
                if b >= 2:
                    dve.wait_ge(y_psum, NT * (b - 1))
                dve.tensor_tensor(hm[:, b % 2, 2 * k:2 * k + 2], bank[H_BANK + k][:, :].rearrange("p (m t) -> p m t", m=2),
                                  mask_rows[:, b % 2].rearrange("p (a t) -> p a t", a=1).broadcast_to([P, 2, T]), ALU.mult).then_inc(hm_ready, 1)

            def residual(i):
                dve.wait_ge(y_psum, i + 1)
                dve.wait_ge(x_loaded[i // NT], 16)
                dve.wait_ge(grec_ready, i // NT + 1)
                dve.scalar_tensor_tensor(x_nat[:, i], bank[Y_BANK + i % 2][:, 0:C], grec[:, i:i + 1], x_nat[:, i],
                                         ALU.mult, ALU.add).then_inc(x1_ready, 1)

            def thresholds():
                dve.wait_ge(wtot_psum, 1)
                dve.tensor_scalar(thr[:, 0], bank[WT_BANK][:, 0:2], 1.0 / (DFF * C), 0.7, ALU.mult, ALU.mult).then_inc(thr_ready, 1)
                dve.wait_ge(thr_ready, 1)
                dve.tensor_scalar(thr[:, 1], thr[:, 0], -1.0, None, ALU.mult).then_inc(thr_ready, 1)

            def negatives(k):
                dve.wait_ge(thr_ready, 2)
                if k:
                    dve.wait_ge(qT_psum, 4)
                flat_w = (w1_nat if k == 0 else w2_nat)[:, :, :].rearrange("p a b -> p (a b)")
                dve.tensor_scalar(neg_part[:, :], flat_w, thr[:, 1, k:k + 1], None, ALU.is_le).then_inc(neg_ready, 1)

            def positives(k):
                dve.wait_ge(thr_ready, 2)
                flat_w = (w1_nat if k == 0 else w2_nat)[:, :, :].rearrange("p a b -> p (a b)")
                flat_pos = (pos1 if k == 0 else pos2)[:, :, :].rearrange("p a b -> p (a b)")
                dve.tensor_scalar(flat_pos, flat_w, thr[:, 0, k:k + 1], None, ALU.is_ge).then_inc(pos_ready, 1)

            def ffn_input(b):
                dve.wait_ge(tanh_ready, b + 1)
                dve.wait_ge(ratio_ready[1], b + 1)
                dve.scalar_tensor_tensor(sig[:, b], sig[:, b], 1.0, nd[1][:, b, :, 0, :], ALU.add, ALU.mult).then_inc(xin_ready, 1)

            def result(i):
                dve.wait_ge(o_psum, i + 1)
                dve.wait_ge(x1b_ready, i + 1)
                if i >= 2:
                    dve.wait_ge(out_stored[i % 2], 16 * (i // 2))
                dve.tensor_tensor(outb[:, i % 2], bank[Y_BANK + i % 2][:, 0:C], x1b[:, i], ALU.add).then_inc(out_ready, 1)

            scales()
            scale_values(dve, 0)
            vectors()
            keys_values(0)
            clip_euk(dve, 0, 0)
            decays()
            forward(0, 0, 0)
            forward(0, 0, 1)
            scale_by(dve, 0, 0, 0)
            backward(0, 0, 0)
            backward(0, 0, 1)
            add_den(dve, 0, 0)
            keys_values(1)
            add_num(dve, 0, 0)
            times_values(dve, 1)
            num_times_rec(dve, 0, 0)
            forward(0, 1, 0)
            keys_values(2)
            forward(0, 1, 1)
            backward(0, 1, 0)
            keys_values(3)
            clip_euk(dve, 0, 1)
            forward(0, 2, 0)
            backward(0, 1, 1)
            forward(0, 2, 1)
            add_den(dve, 0, 1)
            ratio(0, 0)
            backward(0, 2, 0)
            thresholds()
            forward(0, 3, 0)
            positives(0)
            clip_euk(dve, 0, 2)
            forward(0, 3, 1)
            clip_euk(dve, 0, 3)
            gate(0)
            backward(0, 2, 1)
            negatives(0)
            ratio(0, 1)
            backward(0, 3, 0)
            select_expert(0, 0)
            backward(0, 3, 1)
            gate(1)
            probability(0)
            select_expert(0, 1)
            clip_euk(dve, 1, 0)
            positives(1)
            select_expert(1, 0)
            residual(0)
            clip_euk(dve, 1, 1)
            ratio(0, 2)
            clip_euk(dve, 1, 2)
            add_den(dve, 0, 3)
            residual(1)
            forward(1, 0, 0)
            gate(2)
            forward(1, 0, 1)
            backward(1, 0, 0)
            select_expert(1, 1)
            forward(1, 1, 0)
            backward(1, 0, 1)
            forward(1, 1, 1)
            negatives(1)
            forward(1, 2, 0)
            backward(1, 1, 0)
            ratio(0, 3)
            forward(1, 2, 1)
            backward(1, 1, 1)
            select_expert(2, 0)
            backward(1, 2, 0)
            gate(3)
            backward(1, 2, 1)
            select_expert(2, 1)
            add_den(dve, 1, 2)
            probability(1)
            clip_euk(dve, 1, 3)
            residual(2)
            times_v(dve, 1, 2)
            residual(3)
            select_expert(3, 0)
            probability(2)
            select_expert(3, 1)
            add_num(dve, 1, 2)
            residual(4)
            ratio(1, 0)
            probability(3)
            ffn_input(0)
            add_b2(dve, 0)
            ratio(1, 1)
            xin_low(dve, 0)
            ffn_input(1)
            ratio(1, 2)
            add_b2(dve, 1)
            forward(1, 3, 0)
            add_b2(dve, 2)
            residual(5)
            forward(1, 3, 1)
            backward(1, 3, 0)
            residual(6)
            ffn_input(2)
            residual(7)
            h_low(dve, 0, 2)
            backward(1, 3, 1)
            xin_low(dve, 2)
            add_den(dve, 1, 3)
            h_low(dve, 1, 0)
            add_b2(dve, 5)
            add_b2(dve, 6)
            h_low(dve, 1, 1)
            result(0)
            h_low(dve, 1, 2)
            result(1)
            den_times_rec(dve, 1, 3)
            ratio(1, 3)
            ffn_input(3)
            h_low(dve, 2, 0)
            result(2)
            xin_low(dve, 3)
            result(3)
            h_low(dve, 2, 1)
            h_low(dve, 2, 2)
            h_low(dve, 2, 3)
            h_low(dve, 3, 0)
            h_low(dve, 3, 1)
            result(4)
            h_low(dve, 3, 2)
            h_low(dve, 3, 3)
            result(5)
            result(6)
            result(7)
        @block.tensor
        def _(pe):
            pe.wait_ge(consts_ready, 2)

            def keep_warm(done, count, n):
                if done is None:
                    into = WT_BANK
                else:
                    into = x_bank[3]
                    pe.wait_ge(sig_ready, NB)
                    pe.wait_ge(done, count)
                for _ in range(n):
                    pe.transpose(bank[into][:, 0:P], ident[:, :], ident[:, :])

            def transpose_vectors():
                pe.wait_ge(vec_loaded, 16 * 4)
                pe.transpose(bank[MISC_BANK][:, VEC_AT:VEC_AT + NV], vec_rows[:, :], ident[0:NV, 0:NV]).then_inc(vec_psum, 1)

            def transpose_F(b):
                pe.wait_ge(F_loaded[b], 16)
                if b == 3:
                    pe.wait_ge(FT_ready, 1)
                for c in range(NC):
                    for n in range(NT):
                        mm = pe.transpose(bank[F_bank[b]][:, c * T + n * P:c * T + (n + 1) * P],
                                          F_nat[:, b, n, c * P:(c + 1) * P], ident[:, :])
                mm.then_inc(FT_psum, 1)

            def transpose_x(b):
                pe.wait_ge(x_loaded[b], 16)
                for c in range(NC):
                    for n in range(NT):
                        mm = pe.transpose(bank[x_bank[b]][:, c * T + n * P:c * T + (n + 1) * P],
                                          x_nat[:, NT * b + n, c * P:(c + 1) * P], ident[:, :])
                mm.then_inc(xT_psum, 1)

            def transpose_Wg():
                pe.wait_ge(Wg_loaded, 16)
                pe.wait_ge(vecs_ready, 1)
                for c in range(NC):
                    mm = pe.transpose(bank[MISC_BANK][:, WG_AT + NE * c:WG_AT + NE * (c + 1)], Wg_nat[:, c * P:(c + 1) * P], ident[0:NE, 0:NE])
                pe.wait_ge(b1_loaded, 16)
                mm = pe.transpose(bank[MISC_BANK][:, B1_AT:B1_AT + NF], b1_rows[:, :], ident[0:NF, 0:NF])
                mm.then_inc(Wg_psum, 1)

            def transpose_A(c):
                pe.wait_ge(A_loaded, 16)
                if c == 0:
                    pe.wait_ge(FT_ready, 2)
                else:
                    pe.wait_ge(sig_ready, 1)
                for m in range(NM):
                    mm = pe.transpose(bank[A_bank[c]][:, m * P:(m + 1) * P], A_nat[:, m, c * P:(c + 1) * P], ident[:, :])
                mm.then_inc(A_psum, 1)

            def transpose_B(k):
                pe.wait_ge(B_loaded, 16 * NC)
                pe.wait_ge(sig_ready, k + 2)
                for m in (2 * k, 2 * k + 1):
                    for o in range(NC):
                        at = (m % 2) * C + o * P
                        mm = pe.transpose(bank[B_bank[k]][:, at:at + P], B_nat[:, o].rearrange("p e r -> p (e r)")[:, m::NM], ident[:, :])
                mm.then_inc(B_psum, 1)

            def gate_logits(b):
                pe.wait_ge(ratio_ready[0], b + 1)
                if b == 0:
                    pe.wait_ge(WgT_ready, 1)
                else:
                    pe.wait_ge(logits_ready, b)
                for n in range(NT):
                    at = LOGIT_AT + NE * n
                    for c in range(NC):
                        mm = pe.matmul(bank[MISC_BANK][:, at:at + NE], nd[0][:, b, c, 0, n * P:(n + 1) * P], WgT[:, c],
                                       start=(c == 0), stop=(c == NC - 1))
                mm.then_inc(logits_psum, 1)

            def expert_in(b, k):
                pe.wait_ge(ratio_ready[0], b + 1)
                if b == 0:
                    pe.wait_ge(AT_ready, NC)
                    pe.wait_ge(BT_ready, 1)
                else:
                    pe.wait_ge(hm_ready, 2 * (b - 1) + k + 1)
                for m in (2 * k, 2 * k + 1):
                    for c in range(NC):
                        mm = pe.matmul(bank[H_BANK + k][:, (m % 2) * T:(m % 2 + 1) * T], AT[:, c, m::NM],
                                       nd[0][:, b, c, 0, :], start=(c == 0), stop=(c == NC - 1))
                mm.then_inc(h_psum, 1)

            def transpose_mask(b):
                pe.wait_ge(mask_ready, NT * (b + 1))
                pe.wait_ge(identb_ready, 1)
                if b == 0:
                    pe.wait_ge(FT_ready, NB)
                elif b == 1:
                    pe.wait_ge(AT_ready, 1)
                else:
                    pe.wait_ge(mask_copied, b - 1)
                for n in range(NT):
                    mm = pe.transpose(bank[MASK_BANK + b % 2][:, 0:P].bitcast(BF16)[:, n * P:(n + 1) * P], mask[:, NT * (b % 2) + n], identb[:, :])
                mm.then_inc(mask_psum, 1)

            def expert_out(i):
                b, n = divmod(i, NT)
                pe.wait_ge(hm_ready, 2 * (b + 1))
                if i == 0:
                    pe.wait_ge(BT_ready, 2)
                if i == 1:
                    pe.wait_ge(sig_ready, NB)
                if i >= 2:
                    pe.wait_ge(x1_ready, i - 1)
                for m in range(NM):
                    mm = pe.matmul(bank[Y_BANK + i % 2][:, 0:C], hm[:, b % 2, m, n * P:(n + 1) * P], BT[:, m],
                                   start=(m == 0), stop=(m == NM - 1))
                mm.then_inc(y_psum, 1)

            def weight_totals():
                pe.wait_ge(wsum_ready, 2)
                pe.wait_ge(consts_ready, 3)
                pe.wait_ge(FT_ready, 3)
                pe.matmul(bank[WT_BANK][:, 0:2], ones[:, :], wsum[:, :], start=True, stop=True).then_inc(wtot_psum, 1)

            def transpose_weights(k):
                pe.wait_ge(pos_ready, k // 4 + 1)
                pe.wait_ge(neg_ready, k // 4 + 1)
                pe.wait_ge(identb_ready, 2)
                if k:
                    pe.wait_ge(wT_ready, k)
                for s in range(4):
                    if k < 4:
                        f, c = 4 * (k % 2) + s, k // 2
                        at, pos = f * C + c * P, pos1
                    else:
                        f, c = 2 * (k - 4) + s // 2, s % 2
                        at, pos = c * DFF + f * P, pos2
                    flat_pos = pos[:, :, :].rearrange("p a b -> p (a b)")
                    into = bank[WT_BANK][:, s * P:(s + 1) * P]
                    pe.matmul(into, flat_pos[:, at:at + P], identb[:, :], start=True, stop=False)
                    mm = pe.matmul(into, neg_part[:, at:at + P], minus_identb[:, :], start=False, stop=True)
                mm.then_inc(qT_psum, 1)

            def transpose_x1(b):
                pe.wait_ge(x1_ready, NT * (b + 1))
                if b == 0:
                    pe.wait_ge(logits_ready, NB)
                elif b == 1:
                    pe.wait_ge(wT_ready, 8)
                else:
                    pe.wait_ge(tanh_ready, b - 1)
                for c in range(NC):
                    for n in range(NT):
                        mm = pe.transpose(bank[x1T_bank[b % 2]][:, c * T + n * P:c * T + (n + 1) * P],
                                          x_nat[:, NT * b + n, c * P:(c + 1) * P], ident[:, :])
                mm.then_inc(x1T_psum, 1)

            def hidden(b, j):
                pe.wait_ge(xlo_ready, b + 1)
                if b == 0:
                    pe.wait_ge(hm_ready, 2 * NB)
                    pe.wait_ge(wT_ready, 4)
                else:
                    pe.wait_ge(h32_ready, NF * (b - 1) + 2 * j + 2)
                for f in (2 * j, 2 * j + 1):
                    for c in range(NC):
                        for part in (xin_hi, xin_lo):
                            mm = pe.matmul(bank[j][:, (f % 2) * T:(f % 2 + 1) * T], w1T[:, c, f * P:(f + 1) * P],
                                           part[:, b % 2, c], start=(c == 0 and part is xin_hi),
                                           stop=(c == NC - 1 and part is xin_lo))
                mm.then_inc(g_psum, 1)

            def ffn_out(i):
                b, n = divmod(i, NT)
                if i < 2:
                    pe.wait_ge(x1_ready, NI)
                    pe.wait_ge(wT_ready, 8)
                else:
                    pe.wait_ge(out_ready, i - 1)
                for f in range(NF):
                    pe.wait_ge(hlo_ready[f // 2], b + 1)
                    for part in (h_hi, h_lo):
                        mm = pe.matmul(bank[Y_BANK + n][:, 0:C], part[:, b % 2, f, n * P:(n + 1) * P], w2T[:, f],
                                       start=(f == 0 and part is h_hi), stop=(f == NF - 1 and part is h_lo))
                mm.then_inc(o_psum, 1)

            keep_warm(None, 0, 8)
            transpose_F(0)
            transpose_x(0)
            transpose_vectors()
            transpose_x(1)
            transpose_x(2)
            transpose_x(3)
            transpose_F(1)
            transpose_Wg()
            transpose_F(2)
            transpose_B(0)
            transpose_F(3)
            keep_warm(fwd_done[0], 2, 8)
            keep_warm(bwd_done[0], 4, 8)
            keep_warm(bwd_done[0], 2, 8)
            transpose_A(0)
            transpose_B(1)
            transpose_A(1)
            keep_warm(fwd_done[0], 8, 6)
            keep_warm(fwd_done[0], 10, 4)
            keep_warm(fwd_done[0], 12, 8)
            weight_totals()
            gate_logits(0)
            keep_warm(bwd_done[0], 10, 6)
            keep_warm(fwd_done[0], 14, 6)
            expert_in(0, 0)
            transpose_mask(0)
            expert_in(0, 1)
            keep_warm(bwd_done[0], 12, 2)
            transpose_weights(0)
            gate_logits(1)
            keep_warm(bwd_done[0], 14, 2)
            expert_in(1, 0)
            transpose_weights(1)
            transpose_mask(1)
            expert_out(0)
            transpose_weights(2)
            expert_out(1)
            gate_logits(2)
            transpose_weights(3)
            expert_in(1, 1)
            transpose_mask(2)
            expert_in(2, 0)
            expert_out(2)
            expert_in(2, 1)
            transpose_weights(4)
            expert_out(3)
            transpose_weights(5)
            gate_logits(3)
            transpose_weights(6)
            expert_in(3, 0)
            transpose_weights(7)
            transpose_mask(3)
            transpose_x1(0)
            expert_in(3, 1)
            expert_out(4)
            transpose_x1(1)
            expert_out(5)
            expert_out(6)
            hidden(0, 0)
            hidden(0, 1)
            hidden(0, 2)
            hidden(0, 3)
            transpose_x1(2)
            hidden(1, 0)
            expert_out(7)
            hidden(1, 1)
            transpose_x1(3)
            hidden(1, 2)
            hidden(1, 3)
            ffn_out(0)
            hidden(2, 0)
            ffn_out(1)
            hidden(2, 1)
            hidden(2, 2)
            ffn_out(2)
            hidden(2, 3)
            ffn_out(3)
            hidden(3, 0)
            hidden(3, 1)
            hidden(3, 2)
            hidden(3, 3)
            ffn_out(4)
            ffn_out(5)
            ffn_out(6)
            ffn_out(7)


_INS = ['x', 'fside_BxSxS_0', 'cond_512', 'L0_cond_w', 'L0_cond_u', 'L0_ffn_A', 'L0_ffn_Bw', 'L0_ffn_Wg',
        'L1_cond_w', 'L1_cond_u', 'L1_ffn_w1', 'L1_ffn_b1', 'L1_ffn_w2', 'L1_ffn_b2']
_OUTS = [((4, 256, 256), 'float32')]


def kernel(**inputs):
    import numpy as _np
    import concourse.bacc as _bacc
    from concourse import mybir as _mybir
    from concourse.bass_utils import run_bass_kernel_spmd as _run

    nc = _bacc.Bacc("TRN2", target_bir_lowering=False, num_devices=1)
    arrays, args = {}, []
    for name in _INS:
        a = _np.ascontiguousarray(inputs[name])
        arrays[f"in_{name}_dram"] = a
        args.append(nc.dram_tensor(f"in_{name}_dram", a.shape, _mybir.dt.from_np(a.dtype), kind="ExternalInput").ap())
    for i, (shape, dtype) in enumerate(_OUTS):
        dt = _mybir.dt.from_np(_np.dtype(dtype))
        args.append(nc.dram_tensor(f"out_{i}_dram", shape, dt, kind="ExternalOutput").ap())
    adaln_ffn_kernel(nc, *args)
    r = _run(nc, [arrays], core_ids=[0])
    return r.results[0]["out_0_dram"]
```
